# Optimizing a Trainium2 kernel written in Bass

```python
import numpy as np
import jax
import jax.numpy as jnp

def _softmax(x, axis=-1):
    return jax.nn.softmax(x, axis=axis)

def _gelu(x):
    return jax.nn.gelu(x, approximate=True)

def _silu(x):
    return jax.nn.silu(x)

def _sigmoid(x):
    return jax.nn.sigmoid(x)

def _layernorm(x, axis=-1, eps=1e-05):
    m = jnp.mean(x, axis=axis, keepdims=True)
    v = jnp.var(x, axis=axis, keepdims=True)
    return (x - m) / jnp.sqrt(v + eps)

def _scatter_add(tgt, idx, src, axis=0):
    return tgt.at[idx].add(src)

def _segment_sum(src, seg, n):
    return jax.ops.segment_sum(src, seg, n)
kernel_name = 'mk_prb_d1_jaxref_r8_934f95'

def setup_inputs(seed: int=0):
    np.random.seed(seed)
    _w = jnp.asarray

    def _L0_attn_setup():
        import jax, jax.numpy as jnp
        import numpy as np
        D_MODEL, H, DK, DV = (128, 16, 64, 64)
        key = jax.random.key(seed)
        ks = jax.random.split(key, 9)
        s = lambda fan_in: 1.0 / np.sqrt(fan_in)
        return {'x': jax.random.normal(ks[0], (2, 256, D_MODEL), dtype=jnp.float32), 'Wq': jax.random.uniform(ks[1], (D_MODEL, H * DK), jnp.float32, -s(D_MODEL), s(D_MODEL)), 'bq': jax.random.uniform(ks[2], (H * DK,), jnp.float32, -s(D_MODEL), s(D_MODEL)), 'Wk': jax.random.uniform(ks[3], (D_MODEL, DK), jnp.float32, -s(D_MODEL), s(D_MODEL)), 'bk': jax.random.uniform(ks[4], (DK,), jnp.float32, -s(D_MODEL), s(D_MODEL)), 'Wv': jax.random.uniform(ks[5], (D_MODEL, DV), jnp.float32, -s(D_MODEL), s(D_MODEL)), 'bv': jax.random.uniform(ks[6], (DV,), jnp.float32, -s(D_MODEL), s(D_MODEL)), 'Wo': jax.random.uniform(ks[7], (H * DV, D_MODEL), jnp.float32, -s(H * DV), s(H * DV)), 'bo': jax.random.uniform(ks[8], (D_MODEL,), jnp.float32, -s(H * DV), s(H * DV))}
    _L0_attn_in = _L0_attn_setup()

    def _L0_ffn_setup():
        import jax, jax.numpy as jnp
        import numpy as np
        TOP_K = 2
        EPS = 1e-10
        key = jax.random.key(seed)
        k1, k2, k3, k4 = jax.random.split(key, 4)
        B, S, H, E = (4, 256, 128, 8)
        tokens = jax.random.normal(k1, (B, S, H), dtype=jnp.float32)
        router_w = jax.random.normal(k2, (E, H), dtype=jnp.float32) * (1.0 / np.sqrt(H))
        router_b = jax.random.normal(k3, (E,), dtype=jnp.float32) * 0.01
        expert_weights = jax.random.normal(k4, (E, H, H), dtype=jnp.float32) * (1.0 / np.sqrt(H))
        return {'tokens': tokens, 'router_w': router_w, 'router_b': router_b, 'expert_weights': expert_weights}
    _L0_ffn_in = _L0_ffn_setup()
    _d = {'L0_attn_x': _L0_attn_in['x'], 'L0_attn_Wq': _L0_attn_in['Wq'], 'L0_attn_bq': _L0_attn_in['bq'], 'L0_attn_Wk': _L0_attn_in['Wk'], 'L0_attn_bk': _L0_attn_in['bk'], 'L0_attn_Wv': _L0_attn_in['Wv'], 'L0_attn_bv': _L0_attn_in['bv'], 'L0_attn_Wo': _L0_attn_in['Wo'], 'L0_attn_bo': _L0_attn_in['bo'], 'L0_ffn_router_w': _L0_ffn_in['router_w'], 'L0_ffn_router_b': _L0_ffn_in['router_b'], 'L0_ffn_expert_weights': _L0_ffn_in['expert_weights']}
    _x0 = _d['L0_attn_x']
    _d['L0_attn_x'] = jax.random.normal(jax.random.fold_in(jax.random.key(seed), 1), (8, 512, 128), dtype=_x0.dtype)
    del _x0
    return _d

def reference(L0_attn_x, L0_attn_Wq, L0_attn_bq, L0_attn_Wk, L0_attn_bk, L0_attn_Wv, L0_attn_bv, L0_attn_Wo, L0_attn_bo, L0_ffn_router_w, L0_ffn_router_b, L0_ffn_expert_weights):

    def _L0_attn_ref(x, Wq, bq, Wk, bk, Wv, bv, Wo, bo):
        import jax, jax.numpy as jnp
        import numpy as np
        D_MODEL, H, DK, DV = (128, 16, 64, 64)
        B, S, _ = x.shape
        q = (x @ Wq + bq).reshape(B, S, H, DK)
        k = x @ Wk + bk
        v = x @ Wv + bv
        scores = jnp.einsum('bshd,btd->bhst', q, k) / np.sqrt(DK).astype(x.dtype)
        w = jax.nn.softmax(scores, axis=-1)
        out = jnp.einsum('bhst,btd->bshd', w, v).reshape(B, S, H * DV)
        return out @ Wo + bo

    def _L0_ffn_ref(tokens, router_w, router_b, expert_weights):
        import jax, jax.numpy as jnp
        import numpy as np
        TOP_K = 2
        EPS = 1e-10
        B, S, H = tokens.shape
        E = expert_weights.shape[0]
        logits = jnp.einsum('bsh,eh->bse', tokens, router_w) + router_b
        probs = jax.nn.softmax(logits, axis=-1)
        top_p, top_i = jax.lax.top_k(probs, TOP_K)
        w = top_p / (jnp.sum(top_p, axis=-1, keepdims=True) + EPS)
        x = tokens.reshape(-1, H)
        idx = top_i.reshape(-1, TOP_K)
        wf = w.reshape(-1, TOP_K)
        y_all = jnp.einsum('nh,ehd->ned', x, expert_weights)
        y_k = jnp.take_along_axis(y_all, idx[:, :, None], axis=1)
        out = jnp.einsum('nk,nkh->nh', wf, y_k)
        acc = jnp.clip(jnp.sum(wf, axis=-1), EPS, None)
        out = (out / acc[:, None]).reshape(B, S, H)
        scale = 1.0 + jnp.sum(w, axis=-1, keepdims=True) * EPS
        return out * scale
    x = L0_attn_x
    xn = _layernorm(x, axis=-1)
    x = x + _L0_attn_ref(xn, L0_attn_Wq, L0_attn_bq, L0_attn_Wk, L0_attn_bk, L0_attn_Wv, L0_attn_bv, L0_attn_Wo, L0_attn_bo) + _L0_ffn_ref(xn, L0_ffn_router_w, L0_ffn_router_b, L0_ffn_expert_weights)
    return x

_drawn_inputs = setup_inputs


def setup_inputs(seed=0):
    import zlib

    import numpy as np

    out = dict(_drawn_inputs(seed))
    spreads = {}
    factors = {'L0_attn_Wq': 6.265,
     'L0_attn_bq': 8.0,
     'L0_attn_Wk': 6.35,
     'L0_attn_bk': 64.0,
     'L0_attn_Wv': 3.809,
     'L0_attn_bo': 3.744,
     'L0_attn_bv': 2.719}
    for name, (base, spread) in spreads.items():
        noise = np.random.default_rng([zlib.crc32(name.encode()), seed]).standard_normal(out[name].shape)
        drawn = base * np.exp(spread * noise) if base else spread * noise
        out[name] = jnp.asarray(drawn.astype(out[name].dtype))
    for name, factor in factors.items():
        out[name] = (out[name] * factor).astype(out[name].dtype)
    return out
```

```python
from contextlib import ExitStack

import concourse.bass as bass
from concourse import mybir

F32 = mybir.dt.float32
F32R = mybir.dt.float32r
F16 = mybir.dt.float16
ALU = mybir.AluOpType
ACT = mybir.ActivationFunctionType
AX = mybir.AxisListType

P = 128
B, S, D = 8, 512, 128
H, DK = 16, 64
EXPERTS = 8
T = S // P
PAIRS = H // 2
UNITS = B * H
HALF = EXPERTS // 2
VW = 2 * DK + 1
VS = VW + 1
LN_EPS = 1e-5
MOE_EPS = 1e-10
EXP_TOP = 8.0
LN_EXP_TOP = 2.0794415416798357
VALUE_TOP = 1024.0
SCALE = float(DK) ** -0.5
GATE_STEPS = 30

KK0 = 0
VV0 = KK0 + 2 * DK
RT0 = VV0 + 2 * DK
WQ0 = RT0 + EXPERTS
WE0 = WQ0 + H * DK
WCOLS = WE0 + EXPERTS * D
BQ0, BK0, BV0, BO0 = 0, PAIRS, PAIRS + 1, PAIRS + 2
RB0 = BO0 + 1
RANK0 = RB0 + EXPERTS
CCOLS = RANK0 + EXPERTS


def live(b, h, ahead):
    return not isinstance(b, int) or 0 <= H * b + h + ahead < UNITS


def build(nc, x, weights, wo, columns, out):
    ctx = ExitStack()
    with ctx:
        def sb(name, shape, dt):
            return ctx.enter_context(nc.sbuf_tensor(name, shape, dt))

        def ps(name, shape, dt=F32):
            return ctx.enter_context(nc.psum_tensor(name, shape, dt))

        def sem(name):
            return ctx.enter_context(nc.semaphore(name))

        w_raw = sb("w_raw", [P, WCOLS], F32)
        w_hi = sb("w_hi", [P, WCOLS], F32R)
        w_lo = sb("w_lo", [P, WCOLS], F32R)
        wo_sb = sb("wo_sb", [P, PAIRS * D], F32)
        cols = sb("cols", [P, CCOLS], F32)
        ident = sb("ident", [P, P], F32)
        exp_bias = sb("exp_bias", [P, 1], F32)
        x_sb = sb("x_sb", [P, B * T * D], F32)
        stats = sb("stats", [P, B * T, 6], F32)
        moments = sb("moments", [P, B * T * 2], F32)
        mean_all = sb("mean_all", [P, B * T], F32)
        var_eps = sb("var_eps", [P, B * T], F32)
        std = sb("std", [P, B * T], F32)
        rstd0 = sb("rstd0", [P, B * T], F32)
        newton = sb("newton", [P, 2, B * T], F32)
        rstd = sb("rstd", [P, B * T], F32)
        xn = sb("xn", [P, T, D], F32)
        xt_hi = sb("xt_hi", [P, S], F32R)
        xt_lo = sb("xt_lo", [P, S], F32R)
        k_hi_next = sb("k_hi_next", [P, S], F32R)
        k_lo_next = sb("k_lo_next", [P, S], F32R)
        k_hi = sb("k_hi", [P, S], F32R)
        k_lo_even = sb("k_lo_even", [P, S], F32R)
        k_lo_odd = sb("k_lo_odd", [P, S], F32R)
        v_t = sb("v_t", [P, S], F32)
        v_absmax = sb("v_absmax", [P, 1], F32)
        v_unit_next = sb("v_unit_next", [P, 1], F32)
        v_unit = sb("v_unit", [P, 1], F32)
        v_scale = sb("v_scale", [P, 1], F32)
        v_scaled = sb("v_scaled", [P, S], F32)
        v_next = sb("v_next", [P, T * VS], F16)
        v_cur = sb("v_cur", [P, T * VS], F16)
        q_even = sb("q_even", [P, 4, S], F32R)
        q_odd = sb("q_odd", [P, 4, S], F32R)
        q_lo = sb("q_lo", [P, 2, S], F32R)
        q_full_even = sb("q_full_even", [P, 4, S], F32R)
        q_full_odd = sb("q_full_odd", [P, 4, S], F32R)
        neg_max = sb("neg_max", [P, 4, T], F32)
        shift_rows = sb("shift_rows", [T, 2, P], F32R)
        e_hi = sb("e_hi", [P, 4, T, S], F16)
        e_lo = sb("e_lo", [P, 4, T, S], F16)
        e_full = sb("e_full", [P, T, S], F32)
        recip = sb("recip", [P, 2, T], F32)
        o_parts = sb("o_parts", [P, 2, T, 2 * DK], F32)
        o_pair = sb("o_pair", [P, 2, T, 2 * DK], F32)
        o_t = sb("o_t", [P, PAIRS, S], F32)
        attn_t = sb("attn_t", [P, S], F32)
        logits = sb("logits", [P, 2, T, EXPERTS], F32)
        probs = sb("probs", [P, 3, T, EXPERTS], F32)
        onehot = sb("onehot", [P, 2, T, EXPERTS], F32)
        rank = sb("rank", [P, T, EXPERTS], F32)
        small = sb("small", [P, 24, T], F32)
        gate_parts = sb("gate_parts", [P, 2, T, EXPERTS], F32)
        gates = sb("gates", [P, T, EXPERTS], F32)

        score_ps = ps("score_ps", [P, 2, S])
        max_ps = ps("max_ps", [P, 2, S])
        pv_ps = ps("pv_ps", [P, 2, S])
        work_ps = ps("work_ps", [P, S])
        shift_ps = ps("shift_ps", [P, S])

        cols_in, w_in, wo_in = sem("cols_in"), sem("w_in"), sem("wo_in")
        x_in = [sem(f"x_in{i}") for i in range(B)]
        consts_set, ident_set = sem("consts_set"), sem("ident_set")
        w_hi_set, w_lo_set = sem("w_hi_set"), sem("w_lo_set")
        var_set, std_set, ln_step, rstd_set = sem("var_set"), sem("std_set"), sem("ln_step"), sem("rstd_set")
        xn_set, xt_up, xt_hi_set, xt_lo_set = sem("xn_set"), sem("xt_up"), sem("xt_hi_set"), sem("xt_lo_set")
        k_up, k_hi_next_set, k_lo_next_set = sem("k_up"), sem("k_hi_next_set"), sem("k_lo_next_set")
        k_hi_set, k_lo_set = sem("k_hi_set"), sem("k_lo_set")
        v_up, v_t_set, v_step, v_scaled_set = sem("v_up"), sem("v_t_set"), sem("v_step"), sem("v_scaled_set")
        vt_up, v_hi_set, v_next_set, v_cur_set = sem("vt_up"), sem("v_hi_set"), sem("v_next_set"), sem("v_cur_set")
        v_unit_set = sem("v_unit_set")
        router_up, logits_set, shifted_set, exp_logits_set, gate_step = (
            sem("router_up"), sem("logits_set"), sem("shifted_set"), sem("exp_logits_set"), sem("gate_step"))
        gates_set = sem("gates_set")
        experts_up, experts_step = sem("experts_up"), sem("experts_step")
        q_up, q_hi_set, q_lo_set = sem("q_up"), sem("q_hi_set"), sem("q_lo_set")
        q_full_in = [sem("q_full_in0"), sem("q_full_in1")]
        max_up, max_set = sem("max_up"), sem("max_set")
        shift_up, shift_row_set = sem("shift_up"), sem("shift_row_set")
        shift_in = [sem("shift_in0"), sem("shift_in1")]
        scores_up, exp_set, e_lo_set = sem("scores_up"), sem("exp_set"), sem("e_lo_set")
        pv_up, recip_set, o_parts_set, o_pair_set = sem("pv_up"), sem("recip_set"), sem("o_parts_set"), sem("o_pair_set")
        ot_up, ot_set = sem("ot_up"), sem("ot_set")
        wo_up, attn_set, final_up, final_set = sem("wo_up"), sem("attn_set"), sem("final_up"), sem("final_set")
        stored = sem("stored")

        def over_batches(eng, body):
            body(0)
            with eng.Fori(1, B - 1) as b:
                body(b)
            body(B - 1)

        block = ctx.enter_context(nc.Block())

        @block.sync
        def _(sp):
            sp.dma_start(x_sb[:, 0:T * D].rearrange("p (t d) -> p t d", t=T),
                         x[0].rearrange("(t p) d -> p t d", p=P)).then_inc(x_in[0], 16)
            sp.dma_start(cols[:, :], columns).then_inc(cols_in, 16)
            sp.dma_start(w_raw[:, :], weights).then_inc(w_in, 16)
            for i in range(1, B):
                sp.dma_start(x_sb[:, i * T * D:(i + 1) * T * D].rearrange("p (t d) -> p t d", t=T),
                             x[i].rearrange("(t p) d -> p t d", p=P)).then_inc(x_in[i], 16)
            sp.dma_start(wo_sb[:, :], wo).then_inc(wo_in, 16)

            def value(v):
                return v if isinstance(v, int) else sp.snap(v)

            def send_queries(j, p):
                n, m = p % 4, p % 2
                lows = value(j + 1)
                sp.wait_ge(q_lo_set, lows)
                for dst, src in ((q_full_even[0:DK, n, :], q_even[0:DK, n, :]),
                                 (q_full_even[DK:P, n, :], q_lo[0:DK, m, :]),
                                 (q_full_odd[0:DK, n, :], q_lo[DK:P, m, :]),
                                 (q_full_odd[DK:P, n, :], q_odd[DK:P, n, :])):
                    sp.dma_start(dst.bitcast(F32), src.bitcast(F32)).then_inc(q_full_in[m], 16)

            def send_shift(u, h):
                n = (h // 2) % 4
                made = value(u + 1)
                sp.wait_ge(shift_row_set, made)
                row = q_even[DK:DK + 1, n, :] if h % 2 == 0 else q_odd[0:1, n, :]
                sp.dma_start(row.bitcast(F32), shift_rows[:, h % 2, :].bitcast(F32)).then_inc(shift_in[h % 2], 16)

            def store(b):
                made, batch, column = value(b + 1), value(b), value(b * (T * D))
                sp.wait_ge(final_set, made)
                sp.dma_start(out[bass.ds(batch, 1)].rearrange("b (t p) d -> p (b t) d", p=P),
                             x_sb[:, bass.ds(column, T * D)].rearrange("p (t d) -> p t d", t=T)).then_inc(stored, 16)

            send_queries(0, 0)
            send_queries(1, 1)
            send_shift(0, 0)

            def body(b):
                for h in range(H):
                    if h == 6 and live(b, h, -H):
                        store(b - 1)
                    if live(b, h, 1):
                        send_shift(b * H + h + 1, h + 1)
                    if h % 2 == 0 and live(b, h, 4):
                        send_queries(b * PAIRS + h // 2 + 2, h // 2 + 2)

            over_batches(sp, body)
            store(B - 1)
            sp.wait_ge(stored, 16 * B)

        @block.gpsimd
        def _(pool):
            def constants(*fills):
                for n, (dst, number) in enumerate(fills):
                    nc.gpsimd.memset(dst, number).then_inc(consts_set, 1)
                    pool.wait_ge(consts_set, n + 1)

            constants((ident[:, :], 0.0), (exp_bias[:, :], LN_EXP_TOP),
                      (k_lo_even[DK:P, :].bitcast(F32), 0.0), (k_lo_even[DK:DK + 1, :].bitcast(F32), 1.0),
                      (k_lo_odd[0:DK, :].bitcast(F32), 0.0), (k_lo_odd[0:1, :].bitcast(F32), 1.0),
                      (v_next[:, :], 1.0))
            nc.gpsimd.affine_select(out=ident[:, :], in_=ident[:, :], compare_op=ALU.not_equal, fill=1.0,
                                    base=0, pattern=[[-1, P]], channel_multiplier=1).then_inc(ident_set, 1)

            def low_exponentials(u, h, tt):
                pool.wait_ge(exp_set, u * T + (tt + 1))
                nc.gpsimd.tensor_tensor(e_lo[:, h % 4, tt, :], e_full[:, tt, :], e_hi[:, h % 4, tt, :],
                                        ALU.subtract).then_inc(e_lo_set, 1)

            def add_parts(u, h, bank):
                pool.wait_ge(o_parts_set, u * 2 + (bank + 1))
                tiles = slice(2 * bank, 2 * bank + 2)
                head = slice((h % 2) * DK, (h % 2) * DK + DK)
                nc.gpsimd.tensor_tensor(o_pair[:, (h // 2) % 2, tiles, head], o_parts[:, h % 2, tiles, 0:DK],
                                        o_parts[:, h % 2, tiles, DK:2 * DK], ALU.add).then_inc(o_pair_set, 1)

            def slot(b, h):
                u = b * H + h
                if live(b, h, -3):
                    add_parts(u - 3, h - 3, 1)
                for tt in range(T):
                    if live(b, h, 0):
                        low_exponentials(u, h, tt)
                    if tt == 1 and live(b, h, -2):
                        add_parts(u - 2, h - 2, 0)

            def body(b):
                for h in range(H):
                    slot(b, h)

            over_batches(pool, body)
            for h in range(H, H + 3):
                slot(B - 1, h)

        @block.scalar
        def _(act):
            act.wait_ge(w_in, 16)
            nc.scalar.activation(w_hi[:, 0:WE0], w_raw[:, 0:WE0], ACT.Copy).then_inc(w_hi_set, 1)
            nc.scalar.activation(w_hi[:, WE0:], w_raw[:, WE0:], ACT.Copy).then_inc(w_hi_set, 1)
            act.wait_ge(var_set, 1)
            nc.scalar.activation(std[:, :], var_eps[:, :], ACT.Sqrt).then_inc(std_set, 1)

            def xt_high(b):
                act.wait_ge(xt_up, b + 1)
                nc.scalar.activation(xt_hi[:, :], work_ps[:, :], ACT.Copy).then_inc(xt_hi_set, 1)

            def k_high(b):
                act.wait_ge(k_up, b + 1)
                nc.scalar.activation(k_hi_next[:, :], work_ps[:, :], ACT.Identity,
                                     bias=cols[:, BK0:BK0 + 1]).then_inc(k_hi_next_set, 1)

            def k_current(b):
                if live(b, 0, -H):
                    act.wait_ge(scores_up, b * (H * T))
                act.wait_ge(k_hi_next_set, b + 1)
                nc.scalar.activation(k_hi[:, :], k_hi_next[:, :].bitcast(F32), ACT.Copy).then_inc(k_hi_set, 1)

            def v_transposed(b):
                act.wait_ge(v_up, b + 1)
                nc.scalar.activation(v_t[:, :], work_ps[:, :], ACT.Identity,
                                     bias=cols[:, BV0:BV0 + 1]).then_inc(v_t_set, 1)

            def v_high(b):
                act.wait_ge(vt_up, b + 1)
                nc.scalar.activation(v_next[:, :].rearrange("p (t c) -> p t c", t=T)[:, :, 0:DK],
                                     work_ps[:, :].rearrange("p (t c) -> p t c", t=T)[:, :, 0:DK],
                                     ACT.Copy).then_inc(v_hi_set, 1)

            def v_unit_current(b):
                nc.scalar.activation(v_unit[:, :], v_unit_next[:, :], ACT.Copy).then_inc(v_unit_set, 1)

            def exp_logits(b):
                act.wait_ge(shifted_set, b + 1)
                nc.scalar.activation(probs[:, 0, :, :], logits[:, 1, :, :], ACT.Exp).then_inc(exp_logits_set, 1)

            def q_high(j, p):
                act.wait_ge(q_up, j + 1)
                for dst in (q_even, q_odd):
                    nc.scalar.activation(dst[:, p % 4, :], work_ps[:, :], ACT.Identity,
                                         bias=cols[:, BQ0 + p % PAIRS:BQ0 + p % PAIRS + 1]).then_inc(q_hi_set, 1)

            def exponentials(u, h, tt):
                act.wait_ge(scores_up, u * T + (tt + 1))
                nc.scalar.activation(e_hi[:, h % 4, tt, :], score_ps[:, tt % 2, :], ACT.Exp,
                                     bias=exp_bias[:, :], scale=SCALE)
                if not (isinstance(u, int) and u == 0):
                    act.wait_ge(e_lo_set, u * T + (tt - T + 1))
                nc.scalar.activation(e_full[:, tt, :], score_ps[:, tt % 2, :], ACT.Exp,
                                     bias=exp_bias[:, :], scale=SCALE).then_inc(exp_set, 1)

            def out_transposed(j, p):
                act.wait_ge(ot_up, j + 1)
                nc.scalar.activation(o_t[:, p % PAIRS, :], work_ps[:, :], ACT.Copy,
                                     scale=v_unit[:, 0:1]).then_inc(ot_set, 1)

            def attention_out(b):
                act.wait_ge(wo_up, b + 1)
                nc.scalar.activation(attn_t[:, :], work_ps[:, :], ACT.Identity,
                                     bias=cols[:, BO0:BO0 + 1]).then_inc(attn_set, 1)

            act.wait_ge(cols_in, 16)
            act.wait_ge(consts_set, 7)
            xt_high(0)
            k_high(0)
            v_transposed(0)
            v_high(0)
            exp_logits(0)
            q_high(0, 0)
            q_high(1, 1)

            def slot(b, h):
                u = b * H + h
                if h == 0:
                    k_current(b)
                for tt in range(T):
                    if live(b, h, 0):
                        exponentials(u, h, tt)
                    if tt == 0:
                        if h == 4 and live(b, h, -H):
                            attention_out(b - 1)
                        if h == 4 and live(b, h, 0):
                            act.wait_ge(ot_up, b * PAIRS)
                            v_unit_current(b)
                            act.wait_ge(v_unit_set, b + 1)
                        if h == 13 and live(b, h, H):
                            v_transposed(b + 1)
                        if h == 14 and live(b, h, H):
                            v_high(b + 1)
                    if tt == 2:
                        if h % 2 == 0 and live(b, h, 4):
                            q_high(b * PAIRS + h // 2 + 2, h // 2 + 2)
                        if h % 2 == 1 and live(b, h, -5):
                            out_transposed(b * PAIRS + (h - 5) // 2, (h - 5) // 2)
                    if tt == 3:
                        if h == 11 and live(b, h, H):
                            xt_high(b + 1)
                        if h == 12 and live(b, h, H):
                            k_high(b + 1)
                        if h == 15 and live(b, h, H):
                            exp_logits(b + 1)

            def body(b):
                for h in range(H):
                    slot(b, h)

            over_batches(act, body)
            for h in range(H, H + 4):
                slot(B - 1, h)
            attention_out(B - 1)

        @block.tensor
        def _(pe):
            reader = [None]

            def work_bank(next_reader, value):
                if reader[0] is not None:
                    pe.wait_ge(*reader[0])
                reader[0] = (next_reader, value)

            def product(dst, stationary, moving, sem_):
                (s_hi, s_lo), (m_hi, m_lo) = stationary, moving
                nc.tensor.matmul(dst, s_hi, m_hi, start=True, stop=False)
                nc.tensor.matmul(dst, s_hi, m_lo, start=False, stop=False)
                last = nc.tensor.matmul(dst, s_lo, m_hi, start=False, stop=True)
                if sem_ is not None:
                    last.then_inc(sem_, 1)

            def weight(a, n):
                return w_hi[:, a:a + n], w_lo[:, a:a + n]

            def tokens(a, n):
                return xt_hi[:, a:a + n], xt_lo[:, a:a + n]

            def transpose_xn(b):
                work_bank(xt_lo_set, b + 1)
                pe.wait_ge(xn_set, b + 1)
                for t in range(T):
                    last = nc.tensor.transpose(work_ps[:, t * P:(t + 1) * P], xn[:, t, :], ident[:, :])
                last.then_inc(xt_up, 1)

            def project_k(b):
                work_bank(k_lo_next_set, b + 1)
                pe.wait_ge(xt_hi_set, b + 1)
                pe.wait_ge(xt_lo_set, b + 1)
                product(work_ps[:, :], weight(KK0, 2 * DK), tokens(0, S), k_up)

            def project_v(b):
                work_bank(v_t_set, b + 1)
                product(work_ps[:, :], weight(VV0, 2 * DK), tokens(0, S), v_up)

            def transpose_v(b):
                work_bank(v_next_set, b + 1)
                pe.wait_ge(v_scaled_set, b + 1)
                for t in range(T):
                    last = nc.tensor.transpose(work_ps[:, t * P:(t + 1) * P], v_scaled[:, t * P:(t + 1) * P],
                                               ident[:, :])
                last.then_inc(vt_up, 1)

            def route(b):
                work_bank(logits_set, b + 1)
                for t in range(T):
                    product(work_ps[:, t * EXPERTS:(t + 1) * EXPERTS], tokens(t * P, P), weight(RT0, EXPERTS),
                            router_up if t == T - 1 else None)

            def project_q(j, p, b_next):
                work_bank(q_lo_set, j + 1)
                if p % PAIRS == 0:
                    pe.wait_ge(xt_hi_set, b_next + 1)
                    pe.wait_ge(xt_lo_set, b_next + 1)
                product(work_ps[:, :], weight(WQ0 + (p % PAIRS) * P, P), tokens(0, S), q_up)

            def experts(b, item):
                t, half = item // 2, item % 2
                work_bank(experts_step, (b * (2 * T) + (item + 1)) * HALF)
                product(work_ps[:, :], tokens(t * P, P), weight(WE0 + half * S, S), experts_up)

            def maxima(u, h, st):
                j2 = (h // 2) % 2
                if st == 0:
                    pe.wait_ge(q_full_in[j2], q_full_value(u, h))
                if not (isinstance(u, int) and u * T + st < 2):
                    pe.wait_ge(max_set, u * T + (st - 1))
                q = q_full_even if h % 2 == 0 else q_full_odd
                k = k_hi_next if h % H < 2 else k_hi
                nc.tensor.matmul(max_ps[:, st % 2, :], q[:, (h // 2) % 4, st * P:(st + 1) * P], k[:, :],
                                 start=True, stop=True).then_inc(max_up, 1)

            def q_full_value(u, h):
                if isinstance(u, int):
                    return 64 * (u // 4 + 1)
                return (u - h % 4) * 16 + 64

            def shift_row(u, h):
                pe.wait_ge(max_set, u * T + T)
                nc.tensor.transpose(shift_ps[0:T, 0:P], neg_max[:, h % 4, :], ident[:, :]).then_inc(shift_up, 1)

            def scores(u, h, tt):
                if tt == 0:
                    pe.wait_ge(shift_in[h % 2], (u - h % 2) * 8 + 16)
                if not (isinstance(u, int) and u * T + tt < 2):
                    pe.wait_ge(exp_set, u * T + (tt - 1))
                n, keys = (h // 2) % 4, slice(tt * P, (tt + 1) * P)
                full, high, low = ((q_full_even, q_even, k_lo_even) if h % 2 == 0 else (q_full_odd, q_odd, k_lo_odd))
                nc.tensor.matmul(score_ps[:, tt % 2, :], k_hi[:, keys], full[:, n, :], start=True, stop=False)
                nc.tensor.matmul(score_ps[:, tt % 2, :], low[:, keys], high[:, n, :],
                                 start=False, stop=True).then_inc(scores_up, 1)

            def weighted_values(u, h, st):
                bank = st // 2
                if st == 0:
                    pe.wait_ge(e_lo_set, u * T + T)
                if st % 2 == 0 and not (isinstance(u, int) and u == 0):
                    pe.wait_ge(o_parts_set, u * 2 + (bank - 1))
                dst = pv_ps[:, bank, (st % 2) * VS:(st % 2) * VS + VW]
                for tt in range(T):
                    for e in (e_hi, e_lo):
                        last = nc.tensor.matmul(dst, e[:, h % 4, tt, st * P:(st + 1) * P],
                                                v_cur[:, tt * VS:tt * VS + VW],
                                                start=(tt == 0 and e is e_hi), stop=(tt == T - 1 and e is e_lo))
                if st % 2 == 1:
                    last.then_inc(pv_up, 1)

            def transpose_out(j, p):
                work_bank(ot_set, j + 1)
                pe.wait_ge(o_pair_set, j * 4 + 4)
                for t in range(T):
                    last = nc.tensor.transpose(work_ps[:, t * P:(t + 1) * P], o_pair[:, p % 2, t, :], ident[:, :])
                last.then_inc(ot_up, 1)

            def project_out(b):
                work_bank(attn_set, b + 1)
                pe.wait_ge(ot_set, (b + 1) * PAIRS)
                for p in range(PAIRS):
                    last = nc.tensor.matmul(work_ps[:, :], wo_sb[:, p * D:(p + 1) * D], o_t[:, p, :],
                                            start=(p == 0), stop=(p == PAIRS - 1))
                last.then_inc(wo_up, 1)

            def transpose_final(b):
                work_bank(final_set, b + 1)
                pe.wait_ge(attn_set, b + 1)
                for t in range(T):
                    last = nc.tensor.transpose(work_ps[:, t * P:(t + 1) * P], attn_t[:, t * P:(t + 1) * P],
                                               ident[:, :])
                last.then_inc(final_up, 1)

            pe.wait_ge(ident_set, 1)
            transpose_xn(0)
            pe.wait_ge(w_hi_set, 2)
            pe.wait_ge(w_lo_set, 2)
            project_k(0)
            project_v(0)
            transpose_v(0)
            route(0)
            project_q(0, 0, 0)
            project_q(1, 1, 0)
            pe.wait_ge(k_hi_next_set, 1)
            for u in (0, 1):
                for st in range(T):
                    maxima(u, u, st)
            shift_row(0, 0)

            def slot(b, h):
                u = b * H + h
                if h == 0:
                    if live(b, h, -2):
                        weighted_values(u - 2, h - 2, 0)
                    pe.wait_ge(k_hi_set, b + 1)
                    pe.wait_ge(k_lo_set, b + 1)
                if h == 2 and live(b, h, 0):
                    pe.wait_ge(v_cur_set, b + 1)
                if h == 14 and live(b, h, 2):
                    pe.wait_ge(k_hi_next_set, b + 2)
                for tt in range(T):
                    if live(b, h, 0):
                        scores(u, h, tt)
                    if live(b, h, -2) and not (h == 0 and tt == 0):
                        weighted_values(u - 2, h - 2, tt)
                    if live(b, h, 2):
                        maxima(u + 2, h + 2, tt)
                    if tt == 0:
                        if h == 4 and live(b, h, -H):
                            pe.wait_ge(wo_in, 16)
                            project_out(b - 1)
                        if h == 5 and live(b, h, -H):
                            transpose_final(b - 1)
                        if h == 13 and live(b, h, H):
                            project_v(b + 1)
                        if h == 14 and live(b, h, H):
                            transpose_v(b + 1)
                    if tt == 1 and live(b, h, 1):
                        shift_row(u + 1, h + 1)
                    if tt == 2:
                        if h % 2 == 0 and live(b, h, 4):
                            project_q(b * PAIRS + h // 2 + 2, h // 2 + 2, b + 1)
                        if h % 2 == 1 and live(b, h, -5):
                            transpose_out(b * PAIRS + (h - 5) // 2, (h - 5) // 2)
                    if tt == 3:
                        if 1 <= h <= EXPERTS and live(b, h, 0):
                            experts(b, h - 1)
                        if h == 11 and live(b, h, H):
                            transpose_xn(b + 1)
                        if h == 12 and live(b, h, H):
                            project_k(b + 1)
                        if h == 14 and live(b, h, H):
                            route(b + 1)

            def body(b):
                reader[0] = (logits_set, b + 1)
                if isinstance(b, int) and b == 0:
                    reader[0] = (q_lo_set, 2)
                for h in range(H):
                    slot(b, h)

            over_batches(pe, body)
            for h in range(H, H + 4):
                slot(B - 1, h)
            project_out(B - 1)
            transpose_final(B - 1)

        @block.vector
        def _(dve):
            gate = [0, 0]

            def step(ins):
                gate[1] += 1
                ins.then_inc(gate_step, 1)
                dve.wait_ge(gate_step, gate[0] * GATE_STEPS + gate[1])

            def wide(a):
                return a.rearrange("p (t o) -> p t o", o=1).broadcast_to([P, T, EXPERTS])

            for i in range(B):
                dve.wait_ge(x_in[i], 16)
                for t in range(T):
                    n = i * T + t
                    nc.vector.bn_stats(stats[:, n, :], x_sb[:, n * D:(n + 1) * D]).then_inc(ln_step, 1)
            for n in range(B * T):
                dve.wait_ge(ln_step, n + 1)
                nc.vector.bn_aggr(moments[:, 2 * n:2 * n + 2], stats[:, n, :]).then_inc(ln_step, 1)
            steps = 2 * B * T
            dve.wait_ge(ln_step, steps)
            pairs = moments[:, :].rearrange("p (n c) -> p n c", c=2)
            nc.vector.tensor_copy(mean_all[:, :], pairs[:, :, 0]).then_inc(ln_step, 1)
            nc.vector.tensor_scalar(var_eps[:, :], pairs[:, :, 1], LN_EPS, None, ALU.add).then_inc(var_set, 1)
            dve.wait_ge(w_hi_set, 1)
            nc.vector.tensor_tensor(w_lo[:, 0:WE0], w_raw[:, 0:WE0], w_hi[:, 0:WE0].bitcast(F32),
                                    ALU.subtract).then_inc(w_lo_set, 1)
            dve.wait_ge(w_hi_set, 2)
            nc.vector.tensor_tensor(w_lo[:, WE0:], w_raw[:, WE0:], w_hi[:, WE0:].bitcast(F32),
                                    ALU.subtract).then_inc(w_lo_set, 1)
            dve.wait_ge(std_set, 1)
            nc.vector.reciprocal(rstd0[:, :], std[:, :]).then_inc(ln_step, 1)
            dve.wait_ge(ln_step, steps + 2)
            nc.vector.tensor_tensor(newton[:, 0, :], rstd0[:, :], rstd0[:, :], ALU.mult).then_inc(ln_step, 1)
            dve.wait_ge(ln_step, steps + 3)
            nc.vector.scalar_tensor_tensor(out=newton[:, 1, :], in0=newton[:, 0, :], scalar=-0.5, in1=var_eps[:, :],
                                           op0=ALU.mult, op1=ALU.mult).then_inc(ln_step, 1)
            dve.wait_ge(ln_step, steps + 4)
            nc.vector.scalar_tensor_tensor(out=rstd[:, :], in0=newton[:, 1, :], scalar=1.5, in1=rstd0[:, :],
                                           op0=ALU.add, op1=ALU.mult).then_inc(rstd_set, 1)
            dve.wait_ge(rstd_set, 1)
            dve.wait_ge(cols_in, 16)
            dve.wait_ge(consts_set, 7)
            for t in range(T):
                nc.vector.tensor_copy(rank[:, t, :], cols[:, RANK0:RANK0 + EXPERTS]).then_inc(ln_step, 1)
            dve.wait_ge(ln_step, steps + 4 + T)

            def normalise(b):
                for t in range(T):
                    n = b * T + t
                    last = nc.vector.tensor_scalar(xn[:, t, :], x_sb[:, bass.ds(n * D, D)], mean_all[:, bass.ds(n, 1)],
                                                   rstd[:, bass.ds(n, 1)], ALU.subtract, ALU.mult)
                last.then_inc(xn_set, 1)

            def xt_low(b):
                dve.wait_ge(xt_hi_set, b + 1)
                nc.vector.tensor_tensor(xt_lo[:, :], work_ps[:, :], xt_hi[:, :].bitcast(F32),
                                        ALU.subtract).then_inc(xt_lo_set, 1)

            def k_low(b):
                dve.wait_ge(k_hi_next_set, b + 1)
                nc.vector.scalar_tensor_tensor(out=k_lo_next[:, :], in0=work_ps[:, :], scalar=cols[:, BK0:BK0 + 1],
                                               in1=k_hi_next[:, :].bitcast(F32), op0=ALU.add,
                                               op1=ALU.subtract).then_inc(k_lo_next_set, 1)

            def k_current(b):
                if live(b, 0, -H):
                    dve.wait_ge(scores_up, b * (H * T))
                dve.wait_ge(k_lo_next_set, b + 1)
                nc.vector.tensor_copy(k_lo_even[0:DK, :], k_lo_next[0:DK, :].bitcast(F32))
                nc.vector.tensor_copy(k_lo_odd[DK:P, :], k_lo_next[DK:P, :].bitcast(F32)).then_inc(k_lo_set, 1)

            def scale_v(b):
                dve.wait_ge(v_t_set, b + 1)
                nc.vector.tensor_reduce(v_absmax[:, :], v_t[:, :], AX.X, ALU.max,
                                        apply_absolute_value=True).then_inc(v_step, 1)
                dve.wait_ge(v_step, b * 3 + 1)
                nc.vector.tensor_scalar(v_unit_next[:, :], v_absmax[:, :], 1e-30, 1.0 / VALUE_TOP, ALU.max,
                                        ALU.mult).then_inc(v_step, 1)
                dve.wait_ge(v_step, b * 3 + 2)
                nc.vector.reciprocal(v_scale[:, :], v_unit_next[:, :]).then_inc(v_step, 1)
                dve.wait_ge(v_step, b * 3 + 3)
                nc.vector.tensor_scalar(v_scaled[:, :], v_t[:, :], v_scale[:, 0:1], None,
                                        ALU.mult).then_inc(v_scaled_set, 1)

            def v_low(b):
                dve.wait_ge(v_hi_set, b + 1)
                nxt = v_next[:, :].rearrange("p (t c) -> p t c", t=T)
                nc.vector.tensor_tensor(nxt[:, :, DK:2 * DK],
                                        work_ps[:, :].rearrange("p (t c) -> p t c", t=T)[:, :, 0:DK],
                                        nxt[:, :, 0:DK], ALU.subtract).then_inc(v_next_set, 1)

            def v_current(b):
                if live(b, 0, -H):
                    dve.wait_ge(pv_up, b * (2 * H))
                nc.vector.tensor_copy(v_cur[:, :], v_next[:, :]).then_inc(v_cur_set, 1)

            def shift_logits(b):
                dve.wait_ge(router_up, b + 1)
                bias = cols[:, RB0:RB0 + EXPERTS].rearrange("p (o e) -> p o e", o=1).broadcast_to([P, T, EXPERTS])
                nc.vector.tensor_tensor(logits[:, 0, :, :],
                                        work_ps[:, 0:T * EXPERTS].rearrange("p (t e) -> p t e", t=T),
                                        bias, ALU.add).then_inc(logits_set, 1)
                dve.wait_ge(logits_set, b + 1)
                gate[:] = b, 0
                step(nc.vector.tensor_reduce(small[:, 0, :], logits[:, 0, :, :], AX.X, ALU.max))
                nc.vector.tensor_tensor(logits[:, 1, :, :], logits[:, 0, :, :], wide(small[:, 0, :]),
                                        ALU.subtract).then_inc(shifted_set, 1)

            def choose(n, source, weight_row):
                step(nc.vector.tensor_reduce(weight_row, source, AX.X, ALU.max))
                step(nc.vector.tensor_tensor(gate_parts[:, 0, :, :], source, wide(weight_row), ALU.is_equal))
                step(nc.vector.tensor_tensor(gate_parts[:, 1, :, :], gate_parts[:, 0, :, :], rank[:, :, :], ALU.mult))
                step(nc.vector.tensor_reduce(small[:, 1, :], gate_parts[:, 1, :, :], AX.X, ALU.max))
                step(nc.vector.tensor_tensor(onehot[:, n, :, :], rank[:, :, :], wide(small[:, 1, :]), ALU.is_equal))

            def make_gates(b):
                dve.wait_ge(exp_logits_set, b + 1)
                gate[0] = b
                row = lambda i: small[:, i, :]
                tt_, ts = nc.vector.tensor_tensor, nc.vector.tensor_scalar
                step(nc.vector.tensor_reduce(row(2), probs[:, 0, :, :], AX.X, ALU.add))
                step(nc.vector.reciprocal(row(3), row(2)))
                step(tt_(probs[:, 1, :, :], probs[:, 0, :, :], wide(row(3)), ALU.mult))
                choose(0, probs[:, 1, :, :], row(4))
                step(nc.vector.scalar_tensor_tensor(out=probs[:, 2, :, :], in0=onehot[:, 0, :, :], scalar=-2.0,
                                                    in1=probs[:, 1, :, :], op0=ALU.mult, op1=ALU.add))
                choose(1, probs[:, 2, :, :], row(5))
                step(tt_(row(6), row(4), row(5), ALU.add))
                step(ts(row(7), row(6), MOE_EPS, None, ALU.add))
                step(nc.vector.reciprocal(row(8), row(7)))
                step(tt_(row(9), row(4), row(8), ALU.mult))
                step(tt_(row(10), row(5), row(8), ALU.mult))
                step(tt_(row(11), row(9), row(10), ALU.add))
                step(ts(row(12), row(11), MOE_EPS, None, ALU.max))
                step(nc.vector.reciprocal(row(13), row(12)))
                step(ts(row(14), row(11), MOE_EPS, 1.0, ALU.mult, ALU.add))
                step(tt_(row(15), row(13), row(14), ALU.mult))
                step(tt_(row(16), row(9), row(15), ALU.mult))
                step(tt_(row(17), row(10), row(15), ALU.mult))
                step(tt_(gate_parts[:, 0, :, :], onehot[:, 0, :, :], wide(row(16)), ALU.mult))
                step(tt_(gate_parts[:, 1, :, :], onehot[:, 1, :, :], wide(row(17)), ALU.mult))
                gate_count = gate[1] + 1
                assert gate_count == GATE_STEPS, gate_count
                step(tt_(gates[:, :, :], gate_parts[:, 0, :, :], gate_parts[:, 1, :, :], ALU.add))

            def experts(b, item):
                t, half = item // 2, item % 2
                dve.wait_ge(experts_up, b * (2 * T) + (item + 1))
                acc = x_sb[:, bass.ds((b * T + t) * D, D)]
                for e in range(HALF):
                    done = (b * (2 * T) + item) * HALF + e
                    if not (isinstance(done, int) and done == 0):
                        dve.wait_ge(experts_step, done)
                    nc.vector.scalar_tensor_tensor(
                        out=acc, in0=work_ps[:, e * D:(e + 1) * D],
                        scalar=gates[:, t, half * HALF + e:half * HALF + e + 1],
                        in1=acc, op0=ALU.mult, op1=ALU.add).then_inc(experts_step, 1)

            def q_low(j, p):
                dve.wait_ge(q_hi_set, j * 2 + 2)
                nc.vector.scalar_tensor_tensor(out=q_lo[:, p % 2, :], in0=work_ps[:, :],
                                               scalar=cols[:, BQ0 + p % PAIRS:BQ0 + p % PAIRS + 1],
                                               in1=q_even[:, p % 4, :].bitcast(F32), op0=ALU.add,
                                               op1=ALU.subtract).then_inc(q_lo_set, 1)

            def maxima(u, h, st):
                dve.wait_ge(max_up, u * T + (st + 1))
                nc.vector.tensor_reduce(neg_max[:, h % 4, st:st + 1], max_ps[:, st % 2, :], AX.X, ALU.max,
                                        negate=True).then_inc(max_set, 1)

            def shift_row(u, h):
                dve.wait_ge(shift_up, u + 1)
                nc.vector.tensor_copy(shift_rows[:, h % 2, :], shift_ps[0:T, 0:P]).then_inc(shift_row_set, 1)

            def normalise_out(u, h, bank):
                dve.wait_ge(pv_up, u * 2 + (bank + 1))
                src = pv_ps[:, bank, 0:2 * VS].rearrange("p (t c) -> p t c", t=2)
                tiles = slice(2 * bank, 2 * bank + 2)
                r = recip[:, h % 2, tiles]
                nc.vector.reciprocal(r.rearrange("p (t o) -> p t o", o=1), src[:, :, 2 * DK:VW]).then_inc(recip_set, 1)
                dve.wait_ge(recip_set, u * 2 + (bank + 1))
                if not (isinstance(u, int) and u < 2):
                    dve.wait_ge(o_pair_set, u * 2 + (bank - 3))
                nc.vector.tensor_tensor(o_parts[:, h % 2, tiles, :], src[:, :, 0:2 * DK],
                                        r.rearrange("p (t o) -> p t o", o=1).broadcast_to([P, 2, 2 * DK]),
                                        ALU.mult).then_inc(o_parts_set, 1)

            def final(b):
                dve.wait_ge(final_up, b + 1)
                acc = x_sb[:, bass.ds(b * (T * D), T * D)]
                nc.vector.tensor_tensor(acc, work_ps[:, :], acc, ALU.add).then_inc(final_set, 1)

            normalise(0)
            xt_low(0)
            k_low(0)
            scale_v(0)
            v_low(0)
            shift_logits(0)
            make_gates(0)
            q_low(0, 0)
            q_low(1, 1)
            for u in (0, 1):
                for st in range(T):
                    maxima(u, u, st)
            shift_row(0, 0)

            def slot(b, h):
                u = b * H + h
                if h == 0:
                    k_current(b)
                if h == 2 and live(b, h, 0):
                    v_current(b)
                if live(b, h, -3):
                    normalise_out(u - 3, h - 3, 1)
                for tt in range(T):
                    if live(b, h, 2):
                        maxima(u + 2, h + 2, tt)
                    if tt == 0:
                        if live(b, h, -2):
                            normalise_out(u - 2, h - 2, 0)
                        if h == 5 and live(b, h, -H):
                            final(b - 1)
                        if h == 13 and live(b, h, H):
                            scale_v(b + 1)
                        if h == 14 and live(b, h, H):
                            v_low(b + 1)
                    if tt == 1 and live(b, h, 1):
                        shift_row(u + 1, h + 1)
                    if tt == 2 and h % 2 == 0 and live(b, h, 4):
                        q_low(b * PAIRS + h // 2 + 2, h // 2 + 2)
                    if tt == 3:
                        if 1 <= h <= EXPERTS and live(b, h, 0):
                            experts(b, h - 1)
                        if h == 9 and live(b, h, H):
                            normalise(b + 1)
                        if h == 11 and live(b, h, H):
                            xt_low(b + 1)
                        if h == 12 and live(b, h, H):
                            k_low(b + 1)
                        if h == 14 and live(b, h, H):
                            shift_logits(b + 1)
                        if h == 15 and live(b, h, H):
                            make_gates(b + 1)

            def body(b):
                for h in range(H):
                    slot(b, h)

            over_batches(dve, body)
            for h in range(H, H + 4):
                slot(B - 1, h)
            final(B - 1)


_OUT = (B, S, D)


def kernel(**inputs):
    import numpy as np
    import concourse.bacc as bacc
    from concourse.bass_utils import run_bass_kernel_spmd

    g = {k.removeprefix("L0_attn_").removeprefix("L0_ffn_"): np.asarray(v) for k, v in inputs.items()}
    weights = np.concatenate([g["Wk"], g["Wk"], g["Wv"], g["Wv"], g["router_w"].T, g["Wq"],
                              g["expert_weights"].transpose(1, 0, 2).reshape(D, EXPERTS * D)], axis=1)
    wo = g["Wo"].reshape(PAIRS, P, D).transpose(1, 0, 2).reshape(P, PAIRS * D)
    columns = np.concatenate([
        g["bq"].reshape(PAIRS, P).T, np.tile(g["bk"], 2)[:, None], np.tile(g["bv"], 2)[:, None], g["bo"][:, None],
        np.broadcast_to(g["router_b"], (P, EXPERTS)),
        np.broadcast_to(np.arange(EXPERTS, 0, -1, dtype=np.float32), (P, EXPERTS))], axis=1)
    arrays = {"x": g["x"], "weights": weights, "wo": wo, "columns": columns}
    arrays = {n: np.ascontiguousarray(a) for n, a in arrays.items()}

    nc = bacc.Bacc("TRN2", target_bir_lowering=False, num_devices=1)
    args = [nc.dram_tensor(f"in_{n}", a.shape, F32, kind="ExternalInput").ap() for n, a in arrays.items()]
    args.append(nc.dram_tensor("out_0", _OUT, F32, kind="ExternalOutput").ap())
    build(nc, *args)
    r = run_bass_kernel_spmd(nc, [{f"in_{n}": a for n, a in arrays.items()}], core_ids=[0])
    return r.results[0]["out_0"]
```

```python
from contextlib import ExitStack

import concourse.bass as bass
from concourse import mybir

F32 = mybir.dt.float32
F32R = mybir.dt.float32r
F16 = mybir.dt.float16
I32 = mybir.dt.int32
ALU = mybir.AluOpType
ACT = mybir.ActivationFunctionType
AX = mybir.AxisListType

P = 128
B, S, D = 8, 512, 128
H, DK = 16, 64
EXPERTS = 8
T = S // P
PAIRS = H // 2
UNITS = B * H
HALF = EXPERTS // 2
VW = 2 * DK + 1
VS = VW + 1
LN_EPS = 1e-5
MOE_EPS = 1e-10
RSQRT_MAGIC = 0x5F3759DF
SIDE_PAIR = 4
NEWTON = 4
EXP_TOP = 8.0
LN_EXP_TOP = 2.0794415416798357
VALUE_TOP = 1024.0
SCALE = float(DK) ** -0.5
LN_STEPS = 2 + 1 + 2 + 3 * NEWTON
GATE_STEPS = 29

KK0 = 0
VV0 = KK0 + 2 * DK
RT0 = VV0 + 2 * DK
WQ0 = RT0 + EXPERTS
WE0 = WQ0 + H * DK
WCOLS = WE0 + EXPERTS * D
BQ0, BK0, BV0, BO0 = 0, PAIRS, PAIRS + 1, PAIRS + 2
RB0 = BO0 + 1
RANK0 = RB0 + EXPERTS
CCOLS = RANK0 + EXPERTS


def live(b, h, ahead):
    return not isinstance(b, int) or 0 <= H * b + h + ahead < UNITS


def build(nc, x, weights, wo, columns, out):
    ctx = ExitStack()
    with ctx:
        def sb(name, shape, dt):
            return ctx.enter_context(nc.sbuf_tensor(name, shape, dt))

        def ps(name, shape, dt=F32):
            return ctx.enter_context(nc.psum_tensor(name, shape, dt))

        def sem(name):
            return ctx.enter_context(nc.semaphore(name))

        w_raw = sb("w_raw", [P, WCOLS], F32)
        w_hi = sb("w_hi", [P, WCOLS], F32R)
        w_lo = sb("w_lo", [P, WCOLS], F32R)
        wo_sb = sb("wo_sb", [P, PAIRS * D], F32)
        cols = sb("cols", [P, CCOLS], F32)
        ident = sb("ident", [P, P], F32)
        x_sb = sb("x_sb", [P, B * T * D], F32)
        stats = sb("stats", [P, T, 6], F32)
        moments = sb("moments", [P, T, 2], F32)
        mean = sb("mean", [P, T], F32)
        var_eps = sb("var_eps", [P, T], F32)
        half_bits = sb("half_bits", [P, T], I32)
        guess = sb("guess", [P, NEWTON + 1, T], I32)
        newton = sb("newton", [P, 2, T], F32)
        xn = sb("xn", [P, T, D], F32)
        xt_hi = sb("xt_hi", [P, S], F32R)
        xt_lo = sb("xt_lo", [P, S], F32R)
        k_hi_next = sb("k_hi_next", [P, S], F32R)
        k_lo_next = sb("k_lo_next", [P, S], F32R)
        k_hi = sb("k_hi", [P, S], F32R)
        k_lo_even = sb("k_lo_even", [P, S], F32R)
        k_lo_odd = sb("k_lo_odd", [P, S], F32R)
        v_t = sb("v_t", [P, S], F32)
        v_absmax = sb("v_absmax", [P, 1], F32)
        v_unit_next = sb("v_unit_next", [P, 1], F32)
        v_unit = sb("v_unit", [P, 1], F32)
        v_scale = sb("v_scale", [P, 1], F32)
        v_scaled = sb("v_scaled", [P, S], F32)
        v_next = sb("v_next", [P, T * VS], F16)
        v_cur = sb("v_cur", [P, T * VS], F16)
        q_even = sb("q_even", [P, 4, S], F32R)
        q_odd = sb("q_odd", [P, 4, S], F32R)
        q_lo = sb("q_lo", [P, 2, S], F32R)
        q_full_even = sb("q_full_even", [P, 4, S], F32R)
        q_full_odd = sb("q_full_odd", [P, 4, S], F32R)
        neg_max = sb("neg_max", [P, 4, T], F32)
        shift_rows = sb("shift_rows", [T, 2, P], F32R)
        e_hi = sb("e_hi", [P, 4, T, S], F16)
        e_lo = sb("e_lo", [P, 4, T, S], F16)
        e_full = sb("e_full", [P, T, S], F32)
        recip = sb("recip", [P, 2, T], F32)
        o_parts = sb("o_parts", [P, 2, T, 2 * DK], F32)
        o_pair = sb("o_pair", [P, 2, T, 2 * DK], F32)
        o_t = sb("o_t", [P, PAIRS, S], F32)
        attn_t = sb("attn_t", [P, S], F32)
        logits = sb("logits", [P, 2, T, EXPERTS], F32)
        probs = sb("probs", [P, 3, T, EXPERTS], F32)
        onehot = sb("onehot", [P, 2, T, EXPERTS], F32)
        rank = sb("rank", [P, T, EXPERTS], F32)
        small = sb("small", [P, 24, T], F32)
        gate_parts = sb("gate_parts", [P, 2, T, EXPERTS], F32)
        gates = sb("gates", [P, T, EXPERTS], F32)

        score_ps = ps("score_ps", [P, 2, S])
        max_ps = ps("max_ps", [P, 2, S])
        pv_ps = ps("pv_ps", [P, 2, S])
        work_ps = ps("work_ps", [P, S])
        side_ps = ps("side_ps", [P, S])

        cols_in, w_in, experts_in, wo_in = sem("cols_in"), sem("w_in"), sem("experts_in"), sem("wo_in")
        x_in = [sem("x_in0"), sem("x_in1")]
        x_rest_in = sem("x_rest_in")
        consts_set, ident_set, rank_set = sem("consts_set"), sem("ident_set"), sem("rank_set")
        w_hi_set, w_lo_set = sem("w_hi_set"), sem("w_lo_set")
        ln_step = sem("ln_step")
        xn_set, xt_up, xt_hi_set, xt_lo_set = sem("xn_set"), sem("xt_up"), sem("xt_hi_set"), sem("xt_lo_set")
        k_up, k_hi_next_set, k_lo_next_set = sem("k_up"), sem("k_hi_next_set"), sem("k_lo_next_set")
        k_hi_set, k_lo_set = sem("k_hi_set"), sem("k_lo_set")
        v_up, v_t_set, v_step, v_scaled_set = sem("v_up"), sem("v_t_set"), sem("v_step"), sem("v_scaled_set")
        vt_up, v_hi_set, v_next_set, v_cur_set = sem("vt_up"), sem("v_hi_set"), sem("v_next_set"), sem("v_cur_set")
        v_unit_set = sem("v_unit_set")
        router_up, logits_set, shifted_set, exp_logits_set, gate_step = (
            sem("router_up"), sem("logits_set"), sem("shifted_set"), sem("exp_logits_set"), sem("gate_step"))
        gates_set = sem("gates_set")
        experts_up, experts_step = sem("experts_up"), sem("experts_step")
        q_up, q_hi_set, q_lo_set = sem("q_up"), sem("q_hi_set"), sem("q_lo_set")
        q_full_in = [sem("q_full_in0"), sem("q_full_in1")]
        max_up, max_set = sem("max_up"), sem("max_set")
        shift_up, shift_row_set = sem("shift_up"), sem("shift_row_set")
        shift_in = [sem("shift_in0"), sem("shift_in1")]
        scores_up, exp_set, e_lo_set = sem("scores_up"), sem("exp_set"), sem("e_lo_set")
        pv_up, recip_set, o_parts_set, o_pair_set = sem("pv_up"), sem("recip_set"), sem("o_parts_set"), sem("o_pair_set")
        ot_up, ot_set = sem("ot_up"), sem("ot_set")
        wo_up, attn_set, final_up, final_set = sem("wo_up"), sem("attn_set"), sem("final_up"), sem("final_set")
        stored = sem("stored")

        def q_bank(p):
            return side_ps if p == SIDE_PAIR else work_ps

        def over_batches(eng, body):
            body(0)
            with eng.Fori(1, B - 1) as b:
                body(b)
            body(B - 1)

        block = ctx.enter_context(nc.Block())

        @block.sync
        def _(sp):
            sp.dma_start(x_sb[:, 0:T * D].rearrange("p (t d) -> p t d", t=T),
                         x[0].rearrange("(t p) d -> p t d", p=P)).then_inc(x_in[0], 16)
            sp.dma_start(cols[:, :], columns).then_inc(cols_in, 16)
            sp.dma_start(w_raw[:, 0:WE0], weights[:, 0:WE0]).then_inc(w_in, 16)
            sp.dma_start(w_raw[:, WE0:], weights[:, WE0:]).then_inc(experts_in, 16)
            for i in range(1, B):
                sp.dma_start(x_sb[:, i * T * D:(i + 1) * T * D].rearrange("p (t d) -> p t d", t=T),
                             x[i].rearrange("(t p) d -> p t d", p=P)).then_inc(x_in[1] if i == 1 else x_rest_in, 16)
            sp.dma_start(wo_sb[:, :], wo).then_inc(wo_in, 16)

            def value(v):
                return v if isinstance(v, int) else sp.snap(v)

            def send_queries(j, p):
                n, m = p % 4, p % 2
                lows = value(j + 1)
                sp.wait_ge(q_lo_set, lows)
                for dst, src in ((q_full_even[0:DK, n, :], q_even[0:DK, n, :]),
                                 (q_full_even[DK:P, n, :], q_lo[0:DK, m, :]),
                                 (q_full_odd[0:DK, n, :], q_lo[DK:P, m, :]),
                                 (q_full_odd[DK:P, n, :], q_odd[DK:P, n, :])):
                    sp.dma_start(dst.bitcast(F32), src.bitcast(F32)).then_inc(q_full_in[m], 16)

            def send_shift(u, h):
                n = (h // 2) % 4
                made = value(u + 1)
                sp.wait_ge(shift_row_set, made)
                row = q_even[DK:DK + 1, n, :] if h % 2 == 0 else q_odd[0:1, n, :]
                sp.dma_start(row.bitcast(F32), shift_rows[:, h % 2, :].bitcast(F32)).then_inc(shift_in[h % 2], 16)

            def store(b):
                made, batch, column = value(b + 1), value(b), value(b * (T * D))
                sp.wait_ge(final_set, made)
                sp.dma_start(out[bass.ds(batch, 1)].rearrange("b (t p) d -> p (b t) d", p=P),
                             x_sb[:, bass.ds(column, T * D)].rearrange("p (t d) -> p t d", t=T)).then_inc(stored, 16)

            send_queries(0, 0)
            send_queries(1, 1)
            send_queries(2, 2)
            send_shift(0, 0)

            def body(b):
                for h in range(H):
                    if h == 5 and live(b, h, -H):
                        store(b - 1)
                    if live(b, h, 1):
                        send_shift(b * H + h + 1, h + 1)
                    if h % 2 == 0 and live(b, h, 4) and not (isinstance(b, int) and b == 0 and h == 0):
                        send_queries(b * PAIRS + h // 2 + 2, h // 2 + 2)

            over_batches(sp, body)
            store(B - 1)
            sp.wait_ge(stored, 16 * B)

        @block.gpsimd
        def _(pool):
            def constants(*fills):
                for n, (dst, number) in enumerate(fills):
                    nc.gpsimd.memset(dst, number).then_inc(consts_set, 1)
                    pool.wait_ge(consts_set, n + 1)

            constants((ident[:, :], 0.0), (k_lo_even[DK:P, :].bitcast(F32), 0.0), (k_lo_even[DK:DK + 1, :].bitcast(F32), 1.0),
                      (k_lo_odd[0:DK, :].bitcast(F32), 0.0), (k_lo_odd[0:1, :].bitcast(F32), 1.0),
                      (v_next[:, :], 1.0))
            nc.gpsimd.affine_select(out=ident[:, :], in_=ident[:, :], compare_op=ALU.not_equal, fill=1.0,
                                    base=0, pattern=[[-1, P]], channel_multiplier=1).then_inc(ident_set, 1)

            def low_exponentials(u, h, tt):
                pool.wait_ge(exp_set, u * T + (tt + 1))
                nc.gpsimd.tensor_tensor(e_lo[:, h % 4, tt, :], e_full[:, tt, :], e_hi[:, h % 4, tt, :],
                                        ALU.subtract).then_inc(e_lo_set, 1)

            def add_parts(u, h, bank):
                pool.wait_ge(o_parts_set, u * 2 + (bank + 1))
                tiles = slice(2 * bank, 2 * bank + 2)
                head = slice((h % 2) * DK, (h % 2) * DK + DK)
                nc.gpsimd.tensor_tensor(o_pair[:, (h // 2) % 2, tiles, head], o_parts[:, h % 2, tiles, 0:DK],
                                        o_parts[:, h % 2, tiles, DK:2 * DK], ALU.add).then_inc(o_pair_set, 1)

            def slot(b, h):
                u = b * H + h
                if live(b, h, -3):
                    add_parts(u - 3, h - 3, 1)
                for tt in range(T):
                    if live(b, h, 0):
                        low_exponentials(u, h, tt)
                    if tt == 1 and live(b, h, -2):
                        add_parts(u - 2, h - 2, 0)

            def body(b):
                for h in range(H):
                    slot(b, h)

            over_batches(pool, body)
            for h in range(H, H + 3):
                slot(B - 1, h)

        @block.scalar
        def _(act):
            act.wait_ge(w_in, 16)
            nc.scalar.activation(w_hi[:, 0:WE0], w_raw[:, 0:WE0], ACT.Copy).then_inc(w_hi_set, 1)

            def xt_high(b):
                act.wait_ge(xt_up, b + 1)
                nc.scalar.activation(xt_hi[:, :], side_ps[:, :], ACT.Copy).then_inc(xt_hi_set, 1)

            def k_high(b):
                act.wait_ge(k_up, b + 1)
                nc.scalar.activation(k_hi_next[:, :], side_ps[:, :], ACT.Identity,
                                     bias=cols[:, BK0:BK0 + 1]).then_inc(k_hi_next_set, 1)

            def k_current(b, half):
                if live(b, 0, -H):
                    act.wait_ge(scores_up, b * (H * T) + (2 * half - 2))
                act.wait_ge(k_hi_next_set, b + 1)
                keys = slice(half * (S // 2), (half + 1) * (S // 2))
                nc.scalar.activation(k_hi[:, keys], k_hi_next[:, keys].bitcast(F32), ACT.Copy).then_inc(k_hi_set, 1)

            def v_transposed(b):
                act.wait_ge(v_up, b + 1)
                nc.scalar.activation(v_t[:, :], side_ps[:, :], ACT.Identity,
                                     bias=cols[:, BV0:BV0 + 1]).then_inc(v_t_set, 1)

            def v_high(b):
                act.wait_ge(vt_up, b + 1)
                nc.scalar.activation(v_next[:, :].rearrange("p (t c) -> p t c", t=T)[:, :, DK:2 * DK],
                                     side_ps[:, :].rearrange("p (t c) -> p t c", t=T)[:, :, 0:DK],
                                     ACT.Copy).then_inc(v_hi_set, 1)

            def v_unit_current(b):
                if live(b, 0, -H):
                    act.wait_ge(ot_set, b * PAIRS)
                act.wait_ge(v_scaled_set, b + 1)
                nc.scalar.activation(v_unit[:, :], v_unit_next[:, :], ACT.Copy).then_inc(v_unit_set, 1)

            def exp_logits(b):
                act.wait_ge(shifted_set, b + 1)
                nc.scalar.activation(probs[:, 0, :, :], logits[:, 1, :, :], ACT.Exp).then_inc(exp_logits_set, 1)

            def q_high(j, p):
                act.wait_ge(q_up, j + 1)
                for dst in (q_even, q_odd):
                    nc.scalar.activation(dst[:, p % 4, :], q_bank(p)[:, :], ACT.Identity,
                                         bias=cols[:, BQ0 + p % PAIRS:BQ0 + p % PAIRS + 1]).then_inc(q_hi_set, 1)

            def exponentials(u, h, tt):
                act.wait_ge(scores_up, u * T + (tt + 1))
                nc.scalar.activation(e_hi[:, h % 4, tt, :], score_ps[:, tt % 2, :], ACT.Exp,
                                     scale=SCALE)
                if not (isinstance(u, int) and u == 0):
                    act.wait_ge(e_lo_set, u * T + (tt - T + 1))
                nc.scalar.activation(e_full[:, tt, :], score_ps[:, tt % 2, :], ACT.Exp,
                                     scale=SCALE).then_inc(exp_set, 1)

            def out_transposed(j, p, b):
                act.wait_ge(ot_up, j + 1)
                if p == 0:
                    act.wait_ge(v_unit_set, b + 1)
                nc.scalar.activation(o_t[:, p % PAIRS, :], work_ps[:, :], ACT.Copy,
                                     scale=v_unit[:, 0:1]).then_inc(ot_set, 1)

            def attention_out(b):
                act.wait_ge(wo_up, b + 1)
                nc.scalar.activation(attn_t[:, :], work_ps[:, :], ACT.Identity,
                                     bias=cols[:, BO0:BO0 + 1]).then_inc(attn_set, 1)

            act.wait_ge(cols_in, 16)
            act.wait_ge(consts_set, 6)
            xt_high(0)
            k_high(0)
            q_high(0, 0)
            v_transposed(0)
            q_high(1, 1)
            v_high(0)
            q_high(2, 2)
            act.wait_ge(experts_in, 16)
            nc.scalar.activation(w_hi[:, WE0:], w_raw[:, WE0:], ACT.Copy).then_inc(w_hi_set, 1)
            exp_logits(0)
            k_current(0, 0)
            k_current(0, 1)

            def slot(b, h):
                u = b * H + h
                for tt in range(T):
                    if live(b, h, 0):
                        exponentials(u, h, tt)
                    if tt % 2 == 1 and h == 15 and live(b, h, 1):
                        k_current(b + 1, tt // 2)
                    if tt == 0 and h == 3 and live(b, h, 0):
                        v_unit_current(b)
                    if tt == 2:
                        if h == 10 and live(b, h, H):
                            xt_high(b + 1)
                        if h == 12 and live(b, h, H):
                            k_high(b + 1)
                        if h == 13 and live(b, h, H):
                            v_transposed(b + 1)
                        if h == 14 and live(b, h, H):
                            v_high(b + 1)
                    if tt == 3:
                        if h == 3 and live(b, h, -H):
                            attention_out(b - 1)
                        if h == 11 and live(b, h, H):
                            exp_logits(b + 1)
                        if h % 2 == 1 and live(b, h, 5):
                            q_high(b * PAIRS + (h + 1) // 2 + 2, (h + 1) // 2 + 2)
                        if h % 2 == 0 and live(b, h, -4):
                            out_transposed(b * PAIRS + (h - 4) // 2, (h - 4) // 2, b)

            def body(b):
                for h in range(H):
                    slot(b, h)

            over_batches(act, body)
            for h in range(H, H + 3):
                slot(B - 1, h)
            attention_out(B - 1)

        @block.tensor
        def _(pe):
            work, side = [None], [None]

            def take(bank, next_reader, value):
                if bank[0] is not None:
                    pe.wait_ge(*bank[0])
                bank[0] = (next_reader, value)

            def product(dst, stationary, moving, sem_):
                (s_hi, s_lo), (m_hi, m_lo) = stationary, moving
                nc.tensor.matmul(dst, s_hi, m_hi, start=True, stop=False)
                nc.tensor.matmul(dst, s_hi, m_lo, start=False, stop=False)
                last = nc.tensor.matmul(dst, s_lo, m_hi, start=False, stop=True)
                if sem_ is not None:
                    last.then_inc(sem_, 1)

            def weight(a, n):
                return w_hi[:, a:a + n], w_lo[:, a:a + n]

            def tokens(a, n):
                return xt_hi[:, a:a + n], xt_lo[:, a:a + n]

            def transpose_xn(b):
                take(side, xt_lo_set, b + 1)
                pe.wait_ge(xn_set, b + 1)
                for t in range(T):
                    last = nc.tensor.transpose(side_ps[:, t * P:(t + 1) * P], xn[:, t, :], ident[:, :])
                last.then_inc(xt_up, 1)

            def project_k(b):
                take(side, k_lo_next_set, b + 1)
                pe.wait_ge(xt_hi_set, b + 1)
                pe.wait_ge(xt_lo_set, b + 1)
                product(side_ps[:, :], weight(KK0, 2 * DK), tokens(0, S), k_up)

            def project_v(b):
                take(side, v_t_set, b + 1)
                product(side_ps[:, :], weight(VV0, 2 * DK), tokens(0, S), v_up)

            def transpose_v(b):
                take(side, v_next_set, b + 1)
                pe.wait_ge(v_scaled_set, b + 1)
                for t in range(T):
                    last = nc.tensor.transpose(side_ps[:, t * P:(t + 1) * P], v_scaled[:, t * P:(t + 1) * P],
                                               ident[:, :])
                last.then_inc(vt_up, 1)

            def route(b):
                take(side, logits_set, b + 1)
                pe.wait_ge(xt_hi_set, b + 1)
                pe.wait_ge(xt_lo_set, b + 1)
                for t in range(T):
                    product(side_ps[:, t * EXPERTS:(t + 1) * EXPERTS], tokens(t * P, P), weight(RT0, EXPERTS),
                            router_up if t == T - 1 else None)

            def project_q(j, p, b_next):
                take(side if q_bank(p) is side_ps else work, q_lo_set, j + 1)
                if p == PAIRS:
                    pe.wait_ge(xt_hi_set, b_next + 1)
                    pe.wait_ge(xt_lo_set, b_next + 1)
                product(q_bank(p)[:, :], weight(WQ0 + (p % PAIRS) * P, P), tokens(0, S), q_up)

            def experts(b, item):
                t, half = item // 2, item % 2
                if isinstance(b, int) and b == 0 and item == 0:
                    pe.wait_ge(w_hi_set, 2)
                    pe.wait_ge(w_lo_set, 2)
                take(side, experts_step, (b * (2 * T) + (item + 1)) * HALF)
                product(side_ps[:, :], tokens(t * P, P), weight(WE0 + half * S, S), experts_up)

            def maxima(u, h, st):
                j2 = (h // 2) % 2
                if st == 0:
                    pe.wait_ge(q_full_in[j2], q_full_value(u, h))
                if not (isinstance(u, int) and u * T + st < 2):
                    pe.wait_ge(max_set, u * T + (st - 1))
                q = q_full_even if h % 2 == 0 else q_full_odd
                k = k_hi_next if h % H < 4 else k_hi
                nc.tensor.matmul(max_ps[:, st % 2, :], q[:, (h // 2) % 4, st * P:(st + 1) * P], k[:, :],
                                 start=True, stop=True).then_inc(max_up, 1)

            def q_full_value(u, h):
                if isinstance(u, int):
                    return 64 * (u // 4 + 1)
                return (u - h % 4) * 16 + 64

            def shift_row(u, h):
                take(side, shift_row_set, u + 1)
                pe.wait_ge(max_set, u * T + T)
                nc.tensor.transpose(side_ps[0:T, 0:P], neg_max[:, h % 4, :], ident[:, :]).then_inc(shift_up, 1)

            def scores(u, h, tt):
                if tt == 0:
                    pe.wait_ge(shift_in[h % 2], (u - h % 2) * 8 + 16)
                if not (isinstance(u, int) and u * T + tt < 2):
                    pe.wait_ge(exp_set, u * T + (tt - 1))
                n, keys = (h // 2) % 4, slice(tt * P, (tt + 1) * P)
                full, high, low = ((q_full_even, q_even, k_lo_even) if h % 2 == 0 else (q_full_odd, q_odd, k_lo_odd))
                nc.tensor.matmul(score_ps[:, tt % 2, :], k_hi[:, keys], full[:, n, :], start=True, stop=False)
                nc.tensor.matmul(score_ps[:, tt % 2, :], low[:, keys], high[:, n, :],
                                 start=False, stop=True).then_inc(scores_up, 1)

            def weighted_values(u, h, st):
                bank = st // 2
                if st == 0:
                    pe.wait_ge(e_lo_set, u * T + T)
                if st % 2 == 0 and not (isinstance(u, int) and u == 0):
                    pe.wait_ge(o_parts_set, u * 2 + (bank - 1))
                a = (st % 2) * VS
                for tt in range(T):
                    queries = slice(st * P, (st + 1) * P)
                    nc.tensor.matmul(pv_ps[:, bank, a:a + VW], e_hi[:, h % 4, tt, queries],
                                     v_cur[:, tt * VS:tt * VS + VW], start=(tt == 0), stop=False)
                    last = nc.tensor.matmul(pv_ps[:, bank, a + DK:a + VW], e_lo[:, h % 4, tt, queries],
                                            v_cur[:, tt * VS + DK:tt * VS + VW], start=False, stop=(tt == T - 1))
                if st % 2 == 1:
                    last.then_inc(pv_up, 1)

            def transpose_out(j, p):
                take(work, ot_set, j + 1)
                pe.wait_ge(o_pair_set, j * 4 + 4)
                for t in range(T):
                    last = nc.tensor.transpose(work_ps[:, t * P:(t + 1) * P], o_pair[:, p % 2, t, :], ident[:, :])
                last.then_inc(ot_up, 1)

            def project_out(b, pairs):
                if pairs[0] == 0:
                    take(work, attn_set, b + 1)
                    pe.wait_ge(ot_set, (b + 1) * PAIRS)
                    pe.wait_ge(wo_in, 16)
                for p in pairs:
                    last = nc.tensor.matmul(work_ps[:, :], wo_sb[:, p * D:(p + 1) * D], o_t[:, p, :],
                                            start=(p == 0), stop=(p == PAIRS - 1))
                if p == PAIRS - 1:
                    last.then_inc(wo_up, 1)

            def transpose_final(b):
                take(work, final_set, b + 1)
                pe.wait_ge(attn_set, b + 1)
                for t in range(T):
                    last = nc.tensor.transpose(work_ps[:, t * P:(t + 1) * P], attn_t[:, t * P:(t + 1) * P],
                                               ident[:, :])
                last.then_inc(final_up, 1)

            pe.wait_ge(ident_set, 1)
            transpose_xn(0)
            pe.wait_ge(w_hi_set, 1)
            pe.wait_ge(w_lo_set, 1)
            project_k(0)
            project_q(0, 0, 0)
            project_v(0)
            project_q(1, 1, 0)
            transpose_v(0)
            project_q(2, 2, 0)
            route(0)
            pe.wait_ge(k_hi_next_set, 1)
            for u in (0, 1):
                for st in range(T):
                    maxima(u, u, st)
            shift_row(0, 0)

            def slot(b, h):
                u = b * H + h
                if h == 0:
                    if live(b, h, -2):
                        weighted_values(u - 2, h - 2, 0)
                if h == 2 and live(b, h, 0):
                    pe.wait_ge(v_cur_set, b + 1)
                if h == 14 and live(b, h, 2):
                    pe.wait_ge(k_hi_next_set, b + 2)
                for tt in range(T):
                    if h == 0 and tt % 2 == 0:
                        pe.wait_ge(k_hi_set, b * 2 + (tt // 2 + 1))
                        pe.wait_ge(k_lo_set, b * 2 + (tt // 2 + 1))
                    if live(b, h, 0):
                        scores(u, h, tt)
                    if tt == 1 and live(b, h, 1):
                        shift_row(u + 1, h + 1)
                    if live(b, h, -2) and not (h == 0 and tt == 0):
                        weighted_values(u - 2, h - 2, tt)
                    if live(b, h, 2):
                        maxima(u + 2, h + 2, tt)
                    if h == 3 and live(b, h, -H):
                        project_out(b - 1, range(2 * tt, 2 * tt + 2))
                    if tt == 0 and h == 5 and live(b, h, -H):
                        transpose_final(b - 1)
                    if tt == 2:
                        if 2 <= h < 2 + EXPERTS and live(b, h, 0):
                            experts(b, h - 2)
                        if h == 10 and live(b, h, H):
                            transpose_xn(b + 1)
                        if h == 11 and live(b, h, H):
                            route(b + 1)
                        if h == 12 and live(b, h, H):
                            project_k(b + 1)
                        if h == 13 and live(b, h, H):
                            project_v(b + 1)
                        if h == 14 and live(b, h, H):
                            transpose_v(b + 1)
                    if tt == 3 and h % 2 == 1 and live(b, h, 5):
                        project_q(b * PAIRS + (h + 1) // 2 + 2, (h + 1) // 2 + 2, b + 1)
                    if tt == 3 and h % 2 == 0 and live(b, h, -4):
                        transpose_out(b * PAIRS + (h - 4) // 2, (h - 4) // 2)

            def body(b):
                if isinstance(b, int) and b == 0:
                    work[0], side[0] = (q_lo_set, 3), (shift_row_set, 1)
                else:
                    work[0], side[0] = (q_lo_set, b * PAIRS + 3), (shift_row_set, b * H + 1)
                for h in range(H):
                    slot(b, h)

            over_batches(pe, body)
            for h in range(H, H + 3):
                slot(B - 1, h)
            project_out(B - 1, range(PAIRS))
            transpose_final(B - 1)

        @block.vector
        def _(dve):
            gate = [0, 0]

            def step(ins):
                gate[1] += 1
                ins.then_inc(gate_step, 1)
                dve.wait_ge(gate_step, gate[0] * GATE_STEPS + gate[1])

            def wide(a):
                return a.rearrange("p (t o) -> p t o", o=1).broadcast_to([P, T, EXPERTS])

            def ln_statistics(b):
                first = b * LN_STEPS
                for t in range(T):
                    last = nc.vector.bn_stats(stats[:, t, :], x_sb[:, bass.ds((b * T + t) * D, D)])
                last.then_inc(ln_step, 1)
                dve.wait_ge(ln_step, first + 1)
                nc.vector.memset(half_bits[:, :], 0)
                for t in range(T):
                    last = nc.vector.bn_aggr(moments[:, t, :], stats[:, t, :])
                last.then_inc(ln_step, 1)
                dve.wait_ge(ln_step, first + 2)
                nc.vector.tensor_copy(mean[:, :], moments[:, :, 0])
                nc.vector.tensor_scalar(var_eps[:, :], moments[:, :, 1], LN_EPS, None, ALU.add).then_inc(ln_step, 1)
                dve.wait_ge(ln_step, first + 3)

            def ln_guess(b):
                first = b * LN_STEPS + 3
                nc.vector.tensor_scalar(half_bits[:, :], var_eps[:, :].bitcast(I32), 1, None,
                                        ALU.arith_shift_right).then_inc(ln_step, 1)
                dve.wait_ge(ln_step, first + 1)
                nc.vector.tensor_scalar(guess[:, 0, :], half_bits[:, :], -1.0, float(RSQRT_MAGIC), ALU.mult,
                                        ALU.add).then_inc(ln_step, 1)
                dve.wait_ge(ln_step, first + 2)

            def ln_newton(b, n):
                first = b * LN_STEPS + 5 + 3 * n
                y, y_next = guess[:, n, :].bitcast(F32), guess[:, n + 1, :].bitcast(F32)
                nc.vector.tensor_tensor(newton[:, 0, :], y, y, ALU.mult).then_inc(ln_step, 1)
                dve.wait_ge(ln_step, first + 1)
                nc.vector.scalar_tensor_tensor(out=newton[:, 1, :], in0=newton[:, 0, :], scalar=-0.5, in1=var_eps[:, :],
                                               op0=ALU.mult, op1=ALU.mult).then_inc(ln_step, 1)
                dve.wait_ge(ln_step, first + 2)
                nc.vector.scalar_tensor_tensor(out=y_next, in0=newton[:, 1, :], scalar=1.5, in1=y,
                                               op0=ALU.add, op1=ALU.mult).then_inc(ln_step, 1)
                dve.wait_ge(ln_step, first + 3)

            def normalise(b):
                for t in range(T):
                    last = nc.vector.tensor_scalar(xn[:, t, :], x_sb[:, bass.ds((b * T + t) * D, D)], mean[:, t:t + 1],
                                                   guess[:, NEWTON, t:t + 1].bitcast(F32), ALU.subtract, ALU.mult)
                last.then_inc(xn_set, 1)

            def low_weights(n, a, z):
                dve.wait_ge(w_hi_set, n)
                nc.vector.tensor_tensor(w_lo[:, a:z], w_raw[:, a:z], w_hi[:, a:z].bitcast(F32),
                                        ALU.subtract).then_inc(w_lo_set, 1)

            def xt_low(b):
                dve.wait_ge(xt_hi_set, b + 1)
                nc.vector.tensor_tensor(xt_lo[:, :], side_ps[:, :], xt_hi[:, :].bitcast(F32),
                                        ALU.subtract).then_inc(xt_lo_set, 1)

            def k_low(b):
                dve.wait_ge(k_hi_next_set, b + 1)
                nc.vector.scalar_tensor_tensor(out=k_lo_next[:, :], in0=side_ps[:, :], scalar=cols[:, BK0:BK0 + 1],
                                               in1=k_hi_next[:, :].bitcast(F32), op0=ALU.add,
                                               op1=ALU.subtract).then_inc(k_lo_next_set, 1)

            def k_current(b, half):
                if live(b, 0, -H):
                    dve.wait_ge(scores_up, b * (H * T) + (2 * half - 2))
                dve.wait_ge(k_lo_next_set, b + 1)
                keys = slice(half * (S // 2), (half + 1) * (S // 2))
                nc.vector.tensor_copy(k_lo_even[0:DK, keys], k_lo_next[0:DK, keys].bitcast(F32))
                nc.vector.tensor_copy(k_lo_odd[DK:P, keys], k_lo_next[DK:P, keys].bitcast(F32)).then_inc(k_lo_set, 1)

            def scale_v(b):
                dve.wait_ge(v_t_set, b + 1)
                nc.vector.tensor_reduce(v_absmax[:, :], v_t[:, :], AX.X, ALU.max,
                                        apply_absolute_value=True).then_inc(v_step, 1)
                dve.wait_ge(v_step, b * 3 + 1)
                nc.vector.tensor_scalar(v_unit_next[:, :], v_absmax[:, :], 1e-30, 1.0 / VALUE_TOP, ALU.max,
                                        ALU.mult).then_inc(v_step, 1)
                dve.wait_ge(v_step, b * 3 + 2)
                nc.vector.reciprocal(v_scale[:, :], v_unit_next[:, :]).then_inc(v_step, 1)
                dve.wait_ge(v_step, b * 3 + 3)
                nc.vector.tensor_scalar(v_scaled[:, :], v_t[:, :], v_scale[:, 0:1], None,
                                        ALU.mult).then_inc(v_scaled_set, 1)

            def v_low(b):
                dve.wait_ge(v_hi_set, b + 1)
                nxt = v_next[:, :].rearrange("p (t c) -> p t c", t=T)
                nc.vector.tensor_tensor(nxt[:, :, 0:DK],
                                        side_ps[:, :].rearrange("p (t c) -> p t c", t=T)[:, :, 0:DK],
                                        nxt[:, :, DK:2 * DK], ALU.subtract).then_inc(v_next_set, 1)

            def v_current(b):
                if live(b, 0, -H):
                    dve.wait_ge(pv_up, b * (2 * H))
                nc.vector.tensor_copy(v_cur[:, :], v_next[:, :]).then_inc(v_cur_set, 1)

            def shift_logits(b):
                dve.wait_ge(router_up, b + 1)
                bias = cols[:, RB0:RB0 + EXPERTS].rearrange("p (o e) -> p o e", o=1).broadcast_to([P, T, EXPERTS])
                nc.vector.tensor_tensor(logits[:, 0, :, :],
                                        side_ps[:, 0:T * EXPERTS].rearrange("p (t e) -> p t e", t=T),
                                        bias, ALU.add).then_inc(logits_set, 1)
                dve.wait_ge(logits_set, b + 1)
                gate[:] = b, 0
                step(nc.vector.tensor_reduce(small[:, 0, :], logits[:, 0, :, :], AX.X, ALU.max))
                nc.vector.tensor_tensor(logits[:, 1, :, :], logits[:, 0, :, :], wide(small[:, 0, :]),
                                        ALU.subtract).then_inc(shifted_set, 1)

            def choose(n, source, weight_row):
                step(nc.vector.tensor_reduce(weight_row, source, AX.X, ALU.max))
                step(nc.vector.tensor_tensor(gate_parts[:, 0, :, :], source, wide(weight_row), ALU.is_equal))
                step(nc.vector.tensor_tensor(gate_parts[:, 1, :, :], gate_parts[:, 0, :, :], rank[:, :, :], ALU.mult))
                step(nc.vector.tensor_reduce(small[:, 1, :], gate_parts[:, 1, :, :], AX.X, ALU.max))
                step(nc.vector.tensor_tensor(onehot[:, n, :, :], rank[:, :, :], wide(small[:, 1, :]), ALU.is_equal))

            def row(i):
                return small[:, i, :]

            def gates_softmax(b):
                dve.wait_ge(exp_logits_set, b + 1)
                gate[:] = b, 1
                step(nc.vector.tensor_reduce(row(2), probs[:, 0, :, :], AX.X, ALU.add))
                step(nc.vector.reciprocal(row(3), row(2)))
                step(nc.vector.tensor_tensor(probs[:, 1, :, :], probs[:, 0, :, :], wide(row(3)), ALU.mult))

            def gates_first(b):
                choose(0, probs[:, 1, :, :], row(4))
                step(nc.vector.scalar_tensor_tensor(out=probs[:, 2, :, :], in0=onehot[:, 0, :, :], scalar=-2.0,
                                                    in1=probs[:, 1, :, :], op0=ALU.mult, op1=ALU.add))

            def gates_second(b):
                choose(1, probs[:, 2, :, :], row(5))

            def gates_weights(b):
                step(nc.vector.tensor_tensor(row(6), row(4), row(5), ALU.add))
                step(nc.vector.tensor_scalar(row(7), row(6), MOE_EPS, None, ALU.add))
                step(nc.vector.reciprocal(row(8), row(7)))
                step(nc.vector.tensor_tensor(row(9), row(4), row(8), ALU.mult))
                step(nc.vector.tensor_tensor(row(10), row(5), row(8), ALU.mult))
                step(nc.vector.tensor_tensor(row(11), row(9), row(10), ALU.add))

            def gates_factor(b):
                step(nc.vector.tensor_scalar(row(12), row(11), MOE_EPS, None, ALU.max))
                step(nc.vector.reciprocal(row(13), row(12)))
                step(nc.vector.tensor_scalar(row(14), row(11), MOE_EPS, 1.0, ALU.mult, ALU.add))
                step(nc.vector.tensor_tensor(row(15), row(13), row(14), ALU.mult))
                step(nc.vector.tensor_tensor(row(16), row(9), row(15), ALU.mult))
                step(nc.vector.tensor_tensor(row(17), row(10), row(15), ALU.mult))

            def gates_spread(b):
                step(nc.vector.tensor_tensor(gate_parts[:, 0, :, :], onehot[:, 0, :, :], wide(row(16)), ALU.mult))
                step(nc.vector.tensor_tensor(gate_parts[:, 1, :, :], onehot[:, 1, :, :], wide(row(17)), ALU.mult))
                nc.vector.tensor_tensor(gates[:, :, :], gate_parts[:, 0, :, :], gate_parts[:, 1, :, :],
                                        ALU.add).then_inc(gates_set, 1)
                dve.wait_ge(gates_set, b + 1)
                assert gate[1] == GATE_STEPS, gate

            def experts(b, item):
                t, half = item // 2, item % 2
                dve.wait_ge(experts_up, b * (2 * T) + (item + 1))
                acc = x_sb[:, bass.ds((b * T + t) * D, D)]
                for e in range(HALF):
                    done = (b * (2 * T) + item) * HALF + e
                    if not (isinstance(done, int) and done == 0):
                        dve.wait_ge(experts_step, done)
                    nc.vector.scalar_tensor_tensor(
                        out=acc, in0=side_ps[:, e * D:(e + 1) * D],
                        scalar=gates[:, t, half * HALF + e:half * HALF + e + 1],
                        in1=acc, op0=ALU.mult, op1=ALU.add).then_inc(experts_step, 1)

            def q_low(j, p):
                dve.wait_ge(q_hi_set, j * 2 + 2)
                nc.vector.scalar_tensor_tensor(out=q_lo[:, p % 2, :], in0=q_bank(p)[:, :],
                                               scalar=cols[:, BQ0 + p % PAIRS:BQ0 + p % PAIRS + 1],
                                               in1=q_even[:, p % 4, :].bitcast(F32), op0=ALU.add,
                                               op1=ALU.subtract).then_inc(q_lo_set, 1)

            def maxima(u, h, st):
                dve.wait_ge(max_up, u * T + (st + 1))
                nc.vector.tensor_reduce(neg_max[:, h % 4, st:st + 1], max_ps[:, st % 2, :], AX.X, ALU.max,
                                        negate=True).then_inc(max_set, 1)

            def shift_row(u, h):
                dve.wait_ge(shift_up, u + 1)
                nc.vector.tensor_scalar(shift_rows[:, h % 2, :], side_ps[0:T, 0:P], LN_EXP_TOP / SCALE, None,
                                        ALU.add).then_inc(shift_row_set, 1)

            def pair_of_tiles(h, bank):
                src = pv_ps[:, bank, 0:2 * VS].rearrange("p (t c) -> p t c", t=2)
                tiles = slice(2 * bank, 2 * bank + 2)
                return src, tiles, recip[:, h % 2, tiles].rearrange("p (t o) -> p t o", o=1)

            def invert_denominators(u, h, bank):
                dve.wait_ge(pv_up, u * 2 + (bank + 1))
                src, _, r = pair_of_tiles(h, bank)
                nc.vector.reciprocal(r, src[:, :, 2 * DK:VW]).then_inc(recip_set, 1)

            def normalise_out(u, h, bank):
                src, tiles, r = pair_of_tiles(h, bank)
                dve.wait_ge(recip_set, u * 2 + (bank + 1))
                if not (isinstance(u, int) and u < 2):
                    dve.wait_ge(o_pair_set, u * 2 + (bank - 3))
                nc.vector.tensor_tensor(o_parts[:, h % 2, tiles, :], src[:, :, 0:2 * DK],
                                        r.broadcast_to([P, 2, 2 * DK]), ALU.mult).then_inc(o_parts_set, 1)

            def final(b):
                dve.wait_ge(final_up, b + 1)
                acc = x_sb[:, bass.ds(b * (T * D), T * D)]
                nc.vector.tensor_tensor(acc, work_ps[:, :], acc, ALU.add).then_inc(final_set, 1)

            dve.wait_ge(x_in[0], 16)
            ln_statistics(0)
            ln_guess(0)
            for n in range(NEWTON):
                ln_newton(0, n)
            normalise(0)
            low_weights(1, 0, WE0)
            dve.wait_ge(cols_in, 16)
            dve.wait_ge(consts_set, 6)
            for t in range(T):
                last = nc.vector.tensor_copy(rank[:, t, :], cols[:, RANK0:RANK0 + EXPERTS])
            last.then_inc(rank_set, 1)
            dve.wait_ge(rank_set, 1)
            xt_low(0)
            k_low(0)
            q_low(0, 0)
            scale_v(0)
            q_low(1, 1)
            v_low(0)
            for st in range(T):
                maxima(0, 0, st)
            q_low(2, 2)
            shift_logits(0)
            for st in range(T):
                maxima(1, 1, st)
            shift_row(0, 0)
            k_current(0, 0)
            k_current(0, 1)

            gate_pieces = (gates_softmax, gates_first, gates_second, gates_weights, gates_factor, gates_spread)
            ahead = {(12, 0): 0, (12, 1): 1, (13, 0): 2, (14, 0): 3, (14, 3): 4, (15, 0): 5}
            at_once = {(0, 0): 0, (0, 1): 1, (0, 2): 2, (1, 0): 3, (1, 1): 4, (1, 2): 5}

            def slot(b, h):
                u = b * H + h
                if h == 2 and live(b, h, 0):
                    v_current(b)
                if live(b, h, -3):
                    invert_denominators(u - 3, h - 3, 1)
                    normalise_out(u - 3, h - 3, 1)
                for tt in range(T):
                    if tt == 1 and live(b, h, 1):
                        shift_row(u + 1, h + 1)
                    if tt == 1 and live(b, h, -2):
                        invert_denominators(u - 2, h - 2, 0)
                    if live(b, h, 2):
                        maxima(u + 2, h + 2, tt)
                    if tt == 1 and live(b, h, -2):
                        normalise_out(u - 2, h - 2, 0)
                    if tt == 0:
                        if h % 2 == 0 and live(b, h, 4) and not (isinstance(b, int) and b == 0 and h == 0):
                            q_low(b * PAIRS + h // 2 + 2, h // 2 + 2)
                        if h == 5 and live(b, h, -H):
                            final(b - 1)
                        if h == 10 and live(b, h, H):
                            normalise(b + 1)
                    if tt == 1:
                        if h % 2 == 1 and h < 2 * NEWTON and live(b, h, H):
                            if h == 1:
                                ln_guess(b + 1)
                            ln_newton(b + 1, h // 2)
                    if tt == 2:
                        if 2 <= h < 2 + EXPERTS and live(b, h, 0):
                            experts(b, h - 2)
                        if isinstance(b, int) and b == 0 and h == 1:
                            low_weights(2, WE0, WCOLS)
                        if h == 10 and live(b, h, H):
                            xt_low(b + 1)
                        if h == 11 and live(b, h, H):
                            shift_logits(b + 1)
                        if h == 12 and live(b, h, H):
                            k_low(b + 1)
                        if h == 13 and live(b, h, H):
                            scale_v(b + 1)
                        if h == 14 and live(b, h, H):
                            v_low(b + 1)
                        if h == 15 and live(b, h, 1):
                            k_current(b + 1, 0)
                    if tt == 3:
                        if h == 0 and live(b, h, H):
                            dve.wait_ge(*((x_in[1], 16) if isinstance(b, int) else (x_rest_in, 16 * (B - 2))))
                            ln_statistics(b + 1)
                        if h == 15 and live(b, h, 1):
                            k_current(b + 1, 1)
                    if (h, tt) in ahead and live(b, h, H):
                        gate_pieces[ahead[h, tt]](b + 1)
                    if isinstance(b, int) and b == 0 and (h, tt) in at_once:
                        gate_pieces[at_once[h, tt]](0)

            def body(b):
                for h in range(H):
                    slot(b, h)

            over_batches(dve, body)
            for h in range(H, H + 3):
                slot(B - 1, h)
            final(B - 1)


_OUT = (B, S, D)


def kernel(**inputs):
    import numpy as np
    import concourse.bacc as bacc
    from concourse.bass_utils import run_bass_kernel_spmd

    g = {k.removeprefix("L0_attn_").removeprefix("L0_ffn_"): np.asarray(v) for k, v in inputs.items()}
    weights = np.concatenate([g["Wk"], g["Wk"], g["Wv"], g["Wv"], g["router_w"].T, g["Wq"],
                              g["expert_weights"].transpose(1, 0, 2).reshape(D, EXPERTS * D)], axis=1)
    wo = g["Wo"].reshape(PAIRS, P, D).transpose(1, 0, 2).reshape(P, PAIRS * D)
    columns = np.concatenate([
        g["bq"].reshape(PAIRS, P).T, np.tile(g["bk"], 2)[:, None], np.tile(g["bv"], 2)[:, None], g["bo"][:, None],
        np.broadcast_to(g["router_b"], (P, EXPERTS)),
        np.broadcast_to(np.arange(EXPERTS, 0, -1, dtype=np.float32), (P, EXPERTS))], axis=1)
    arrays = {"x": g["x"], "weights": weights, "wo": wo, "columns": columns}
    arrays = {n: np.ascontiguousarray(a) for n, a in arrays.items()}

    nc = bacc.Bacc("TRN2", target_bir_lowering=False, num_devices=1)
    args = [nc.dram_tensor(f"in_{n}", a.shape, F32, kind="ExternalInput").ap() for n, a in arrays.items()]
    args.append(nc.dram_tensor("out_0", _OUT, F32, kind="ExternalOutput").ap())
    build(nc, *args)
    r = run_bass_kernel_spmd(nc, [{f"in_{n}": a for n, a in arrays.items()}], core_ids=[0])
    return r.results[0]["out_0"]
```

```python
from contextlib import ExitStack

import concourse.bass as bass
from concourse import mybir

F32 = mybir.dt.float32
F32R = mybir.dt.float32r
F16 = mybir.dt.float16
I32 = mybir.dt.int32
ALU = mybir.AluOpType
ACT = mybir.ActivationFunctionType
AX = mybir.AxisListType

P = 128
B, S, D = 8, 512, 128
H, DK = 16, 64
EXPERTS = 8
T = S // P
PAIRS = H // 2
UNITS = B * H
HALF = EXPERTS // 2
VW = 2 * DK + 1
VS = VW + 1
VR = DK + EXPERTS
OW = DK + 1
LN_EPS = 1e-5
MOE_EPS = 1e-10
RSQRT_MAGIC = 0x5F3759DF
NEWTON = 3
EXP_TOP = 8.0
LN_EXP_TOP = 2.0794415416798357
VALUE_TOP = 1024.0
SCALE = float(DK) ** -0.5
LN_STEPS = 3 + 3 * NEWTON
GATE_STEPS = 24

KK0 = 0
VV0 = KK0 + 2 * DK
WQ0 = VV0 + VR
WE0 = WQ0 + H * DK
WCOLS = WE0 + EXPERTS * D
BQ0, BK0, BV0, BO0 = 0, PAIRS, PAIRS + 1, PAIRS + 2
RANK0 = BO0 + 1
CCOLS = RANK0 + EXPERTS


def live(b, h, ahead):
    return not isinstance(b, int) or 0 <= H * b + h + ahead < UNITS


def build(nc, x, weights, wo, columns, out):
    ctx = ExitStack()
    with ctx:
        def sb(name, shape, dt):
            return ctx.enter_context(nc.sbuf_tensor(name, shape, dt))

        def ps(name, shape, dt=F32):
            return ctx.enter_context(nc.psum_tensor(name, shape, dt))

        def sem(name):
            return ctx.enter_context(nc.semaphore(name))

        w_raw = sb("w_raw", [P, WCOLS], F32)
        w_hi = sb("w_hi", [P, WCOLS], F32R)
        w_lo = sb("w_lo", [P, WCOLS], F32R)
        wo_raw = sb("wo_raw", [P, PAIRS * D], F32)
        wo_hi = sb("wo_hi", [P, PAIRS * D], F32R)
        wo_lo = sb("wo_lo", [P, PAIRS * D], F32R)
        cols = sb("cols", [P, CCOLS], F32)
        ident = sb("ident", [P, P], F32)
        x_sb = sb("x_sb", [P, B * T * D], F32)
        stats = sb("stats", [P, B * T, 6], F32)
        moments = sb("moments", [P, B * T, 2], F32)
        mean = sb("mean", [P, B * T], F32)
        var_eps = sb("var_eps", [P, B * T], F32)
        half_bits = sb("half_bits", [P, B * T], I32)
        guess = sb("guess", [P, NEWTON + 1, B * T], I32)
        newton = sb("newton", [P, 2, B * T], F32)
        mean_cur = sb("mean_cur", [P, T], F32)
        inv_cur = sb("inv_cur", [P, T], F32)
        xn = sb("xn", [P, T, D], F32)
        xt_hi = sb("xt_hi", [P, S], F32R)
        xt_lo = sb("xt_lo", [P, S], F32R)
        k_hi_next = sb("k_hi_next", [P, S], F32R)
        k_lo_next = sb("k_lo_next", [P, S], F32R)
        k_hi = sb("k_hi", [P, S], F32R)
        k_lo_even = sb("k_lo_even", [P, S], F32R)
        k_lo_odd = sb("k_lo_odd", [P, S], F32R)
        v_t = sb("v_t", [VR, S], F32)
        v_absmax = sb("v_absmax", [DK, 1], F32)
        v_unit_next = sb("v_unit_next", [P, 1], F32)
        v_unit = sb("v_unit", [P, 1], F32)
        v_scale = sb("v_scale", [VR, 1], F32)
        v_scaled = sb("v_scaled", [VR, S], F32)
        v_next = sb("v_next", [P, T * VS], F16)
        v_cur = sb("v_cur", [P, T * VS], F16)
        q_even = sb("q_even", [P, 4, S], F32R)
        q_odd = sb("q_odd", [P, 4, S], F32R)
        q_lo = sb("q_lo", [P, 2, S], F32R)
        q_full_even = sb("q_full_even", [P, 4, S], F32R)
        q_full_odd = sb("q_full_odd", [P, 4, S], F32R)
        neg_max = sb("neg_max", [P, 4, T], F32)
        shift_rows = sb("shift_rows", [T, 2, P], F32R)
        e_hi = sb("e_hi", [P, 4, T, S], F16)
        e_lo = sb("e_lo", [P, 4, T, S], F16)
        e_full = sb("e_full", [P, T, S], F32)
        recip = sb("recip", [P, 2, T], F32)
        o_pair = sb("o_pair", [P, 2, T, 2 * DK], F32)
        ot_hi = sb("ot_hi", [P, 2, S], F32R)
        ot_lo = sb("ot_lo", [P, 2, S], F32R)
        attn_t = sb("attn_t", [P, S], F32)
        logits = sb("logits", [P, T, EXPERTS], F32)
        probs = sb("probs", [P, 3, T, EXPERTS], F32)
        onehot = sb("onehot", [P, 2, T, EXPERTS], F32)
        rank = sb("rank", [P, T, EXPERTS], F32)
        small = sb("small", [P, 24, T], F32)
        gate_parts = sb("gate_parts", [P, 2, T, EXPERTS], F32)
        gates = sb("gates", [P, T, EXPERTS], F32)

        score_ps = ps("score_ps", [P, 2, S])
        max_ps = ps("max_ps", [P, 2, S])
        pv_ps = ps("pv_ps", [P, S])
        attn_ps = ps("attn_ps", [P, S])
        work_ps = ps("work_ps", [P, S])
        side_ps = ps("side_ps", [P, S])

        cols_in, w_in, experts_in, wo_in = sem("cols_in"), sem("w_in"), sem("experts_in"), sem("wo_in")
        x_in, x_second_in, x_rest_in = sem("x_in"), sem("x_second_in"), sem("x_rest_in")
        consts_set, ident_set, rank_set = sem("consts_set"), sem("ident_set"), sem("rank_set")
        w_hi_set, w_lo_set = sem("w_hi_set"), sem("w_lo_set")
        stats_set, moments_set = sem("stats_set"), sem("moments_set")
        ln_step, ln_cur_set = sem("ln_step"), sem("ln_cur_set")
        xn_set, xt_up, xt_hi_set, xt_lo_set = sem("xn_set"), sem("xt_up"), sem("xt_hi_set"), sem("xt_lo_set")
        k_up, k_hi_next_set, k_lo_next_set = sem("k_up"), sem("k_hi_next_set"), sem("k_lo_next_set")
        k_hi_set, k_lo_set = sem("k_hi_set"), sem("k_lo_set")
        v_up, v_t_set, v_step, v_scaled_set = sem("v_up"), sem("v_t_set"), sem("v_step"), sem("v_scaled_set")
        vt_up, v_hi_set, v_next_set, v_cur_set = sem("vt_up"), sem("v_hi_set"), sem("v_next_set"), sem("v_cur_set")
        v_unit_in, v_unit_set = sem("v_unit_in"), sem("v_unit_set")
        shifted_set, exp_logits_set, gate_step = sem("shifted_set"), sem("exp_logits_set"), sem("gate_step")
        gates_set = sem("gates_set")
        experts_up, experts_step = sem("experts_up"), sem("experts_step")
        q_up, q_hi_set, q_lo_set = sem("q_up"), sem("q_hi_set"), sem("q_lo_set")
        q_full_in = [sem("q_full_in0"), sem("q_full_in1")]
        max_up, max_set = sem("max_up"), sem("max_set")
        shift_up, shift_row_set = sem("shift_up"), sem("shift_row_set")
        shift_in = [sem("shift_in0"), sem("shift_in1")]
        scores_up, exp_set, e_lo_set = sem("scores_up"), sem("exp_set"), sem("e_lo_set")
        pv_up, recip_set, o_pair_set = sem("pv_up"), sem("recip_set"), sem("o_pair_set")
        ot_up, ot_hi_set, ot_lo_set = sem("ot_up"), sem("ot_hi_set"), sem("ot_lo_set")
        wo_hi_set, wo_lo_set = sem("wo_hi_set"), sem("wo_lo_set")
        wo_up, attn_set, final_up, final_set = sem("wo_up"), sem("attn_set"), sem("final_up"), sem("final_set")
        stored = sem("stored")

        def over_batches(eng, body):
            body(0)
            with eng.Fori(1, B - 1) as b:
                body(b)
            body(B - 1)

        block = ctx.enter_context(nc.Block())

        @block.sync
        def _(sp):
            sp.dma_start(x_sb[:, 0:T * D].rearrange("p (t d) -> p t d", t=T),
                         x[0].rearrange("(t p) d -> p t d", p=P)).then_inc(x_in, 16)
            sp.dma_start(cols[:, :], columns).then_inc(cols_in, 16)
            sp.dma_start(w_raw[:, 0:WE0], weights[:, 0:WE0]).then_inc(w_in, 16)
            sp.dma_start(w_raw[:, WE0:], weights[:, WE0:]).then_inc(experts_in, 16)
            for i in range(1, B):
                sp.dma_start(x_sb[:, i * T * D:(i + 1) * T * D].rearrange("p (t d) -> p t d", t=T),
                             x[i].rearrange("(t p) d -> p t d", p=P)).then_inc(x_second_in if i == 1 else x_rest_in, 16)
            sp.dma_start(wo_raw[:, :], wo).then_inc(wo_in, 16)

            def value(v):
                return v if isinstance(v, int) else sp.snap(v)

            def send_queries(j, p):
                n, m = p % 4, p % 2
                lows = value(j + 1)
                sp.wait_ge(q_lo_set, lows)
                for dst, src in ((q_full_even[0:DK, n, :], q_even[0:DK, n, :]),
                                 (q_full_even[DK:P, n, :], q_lo[0:DK, m, :]),
                                 (q_full_odd[0:DK, n, :], q_lo[DK:P, m, :]),
                                 (q_full_odd[DK:P, n, :], q_even[DK:P, n, :]),
                                 (q_odd[DK:P, n, :], q_even[DK:P, n, :])):
                    sp.dma_start(dst.bitcast(F32), src.bitcast(F32)).then_inc(q_full_in[m], 16)

            def send_shift(u, h):
                n = (h // 2) % 4
                made = value(u + 1)
                sp.wait_ge(shift_row_set, made)
                row = q_even[DK:DK + 1, n, :] if h % 2 == 0 else q_odd[0:1, n, :]
                sp.dma_start(row.bitcast(F32), shift_rows[:, h % 2, :].bitcast(F32)).then_inc(shift_in[h % 2], 16)

            def send_v_unit(b):
                made = value(b * 3 + 2)
                sp.wait_ge(v_step, made)
                sp.dma_start(v_unit_next[DK:P, :], v_unit_next[0:DK, :]).then_inc(v_unit_in, 16)

            def store(b):
                made, batch, column = value(b + 1), value(b), value(b * (T * D))
                sp.wait_ge(final_set, made)
                sp.dma_start(out[bass.ds(batch, 1)].rearrange("b (t p) d -> p (b t) d", p=P),
                             x_sb[:, bass.ds(column, T * D)].rearrange("p (t d) -> p t d", t=T)).then_inc(stored, 16)

            send_queries(0, 0)
            send_queries(1, 1)
            send_shift(0, 0)
            send_queries(2, 2)
            send_v_unit(0)

            def body(b):
                for h in range(H):
                    if h == 7 and live(b, h, -H):
                        store(b - 1)
                    if live(b, h, 1):
                        send_shift(b * H + h + 1, h + 1)
                    if h % 2 == 1 and live(b, h, 5):
                        p = (h + 1) // 2 + 2
                        send_queries(b * PAIRS + p, p)
                    if h == 14 and live(b, h, H):
                        send_v_unit(b + 1)

            over_batches(sp, body)
            store(B - 1)
            sp.wait_ge(stored, 16 * B)

        @block.gpsimd
        def _(pool):
            def constants(*fills):
                for n, (dst, number) in enumerate(fills):
                    nc.gpsimd.memset(dst, number).then_inc(consts_set, 1)
                    pool.wait_ge(consts_set, n + 1)

            constants((ident[:, :], 0.0),
                      (k_lo_even[DK:P, :].bitcast(F32), 0.0), (k_lo_even[DK:DK + 1, :].bitcast(F32), 1.0),
                      (k_lo_odd[0:DK, :].bitcast(F32), 0.0), (k_lo_odd[0:1, :].bitcast(F32), 1.0),
                      (v_next[:, :], 1.0), (v_scale[DK:VR, :], 1.0), (q_odd[0:DK, :, :].bitcast(F32), 0.0))
            nc.gpsimd.affine_select(out=ident[:, :], in_=ident[:, :], compare_op=ALU.not_equal, fill=1.0,
                                    base=0, pattern=[[-1, P]], channel_multiplier=1).then_inc(ident_set, 1)

            def low_exponentials(u, h, tt):
                pool.wait_ge(exp_set, u * T + (tt + 1))
                nc.gpsimd.tensor_tensor(e_lo[:, h % 4, tt, :], e_full[:, tt, :], e_hi[:, h % 4, tt, :],
                                        ALU.subtract).then_inc(e_lo_set, 1)

            def slot(b, h):
                for tt in range(T):
                    if live(b, h, 0):
                        low_exponentials(b * H + h, h, tt)

            def body(b):
                for h in range(H):
                    slot(b, h)

            over_batches(pool, body)

        @block.scalar
        def _(act):
            act.wait_ge(w_in, 16)
            nc.scalar.activation(w_hi[:, 0:WE0], w_raw[:, 0:WE0], ACT.Copy).then_inc(w_hi_set, 1)

            def xt_high(b):
                act.wait_ge(xt_up, b + 1)
                nc.scalar.activation(xt_hi[:, :], work_ps[:, :], ACT.Copy).then_inc(xt_hi_set, 1)

            def k_high(b):
                act.wait_ge(k_up, b + 1)
                nc.scalar.activation(k_hi_next[:, :], side_ps[:, :], ACT.Identity,
                                     bias=cols[:, BK0:BK0 + 1]).then_inc(k_hi_next_set, 1)

            def k_current(b, half):
                if live(b, 0, -H):
                    act.wait_ge(scores_up, b * (H * T) + (2 * half - 2))
                act.wait_ge(k_hi_next_set, b + 1)
                keys = slice(half * (S // 2), (half + 1) * (S // 2))
                nc.scalar.activation(k_hi[:, keys], k_hi_next[:, keys].bitcast(F32), ACT.Copy).then_inc(k_hi_set, 1)

            def v_transposed(b):
                act.wait_ge(v_up, b + 1)
                nc.scalar.activation(v_t[:, :], side_ps[0:VR, :], ACT.Identity,
                                     bias=cols[0:VR, BV0:BV0 + 1]).then_inc(v_t_set, 1)

            def v_high(b):
                act.wait_ge(vt_up, b + 1)
                nc.scalar.activation(v_next[:, :].rearrange("p (t c) -> p t c", t=T)[:, :, DK:2 * DK],
                                     side_ps[:, :].rearrange("p (t c) -> p t c", t=T)[:, :, 0:DK],
                                     ACT.Copy).then_inc(v_hi_set, 1)

            def v_unit_current(b):
                if live(b, 0, -H):
                    act.wait_ge(ot_lo_set, b * PAIRS)
                act.wait_ge(v_unit_in, b * 16 + 16)
                nc.scalar.activation(v_unit[:, :], v_unit_next[:, :], ACT.Copy).then_inc(v_unit_set, 1)

            def exp_logits(b):
                act.wait_ge(shifted_set, b + 1)
                nc.scalar.activation(probs[:, 0, :, :], logits[:, :, :], ACT.Exp).then_inc(exp_logits_set, 1)

            def q_high(j, p):
                act.wait_ge(q_up, j + 1)
                nc.scalar.activation(q_even[:, p % 4, :], work_ps[:, :], ACT.Identity,
                                     bias=cols[:, BQ0 + p % PAIRS:BQ0 + p % PAIRS + 1]).then_inc(q_hi_set, 1)

            def exponentials(u, h, tt):
                act.wait_ge(scores_up, u * T + (tt + 1))
                nc.scalar.activation(e_hi[:, h % 4, tt, :], score_ps[:, tt % 2, :], ACT.Exp,
                                     scale=SCALE)
                if not (isinstance(u, int) and u == 0):
                    act.wait_ge(e_lo_set, u * T + (tt - T + 1))
                nc.scalar.activation(e_full[:, tt, :], score_ps[:, tt % 2, :], ACT.Exp,
                                     scale=SCALE).then_inc(exp_set, 1)

            def out_transposed(j, p, b):
                act.wait_ge(ot_up, j + 1)
                if p == 0:
                    act.wait_ge(v_unit_set, b + 1)
                nc.scalar.activation(ot_hi[:, p % 2, :], work_ps[:, :], ACT.Copy,
                                     scale=v_unit[:, 0:1]).then_inc(ot_hi_set, 1)

            def attention_out(b):
                act.wait_ge(wo_up, b + 1)
                nc.scalar.activation(attn_t[:, :], attn_ps[:, :], ACT.Identity,
                                     bias=cols[:, BO0:BO0 + 1]).then_inc(attn_set, 1)

            act.wait_ge(cols_in, 16)
            xt_high(0)
            q_high(0, 0)
            k_high(0)
            k_current(0, 0)
            k_current(0, 1)
            q_high(1, 1)
            v_transposed(0)
            act.wait_ge(consts_set, 7)
            v_high(0)
            exp_logits(0)
            q_high(2, 2)
            act.wait_ge(experts_in, 16)
            nc.scalar.activation(w_hi[:, WE0:], w_raw[:, WE0:], ACT.Copy).then_inc(w_hi_set, 1)

            def slot(b, h):
                u = b * H + h
                for tt in range(T):
                    if live(b, h, 0):
                        exponentials(u, h, tt)
                    if tt % 2 == 1 and h == 15 and live(b, h, 1):
                        k_current(b + 1, tt // 2)
                    if tt == 0 and h == 4 and live(b, h, 0):
                        v_unit_current(b)
                    if tt == 3 and h == 0 and isinstance(b, int) and b == 0:
                        act.wait_ge(wo_in, 16)
                        nc.scalar.activation(wo_hi[:, :], wo_raw[:, :], ACT.Copy).then_inc(wo_hi_set, 1)
                    if h == 10 and tt == 0 and live(b, h, H):
                        xt_high(b + 1)
                    if h % 2 == 1 and tt == 0 and live(b, h, 5):
                        p = (h + 1) // 2 + 2
                        q_high(b * PAIRS + p, p)
                    if tt == 2:
                        if h == 11 and live(b, h, H):
                            v_transposed(b + 1)
                        if h == 12 and live(b, h, H):
                            v_high(b + 1)
                        if h == 13 and live(b, h, H):
                            k_high(b + 1)
                        if h % 2 == 0 and live(b, h, -4):
                            out_transposed(b * PAIRS + (h - 4) // 2, (h - 4) // 2, b)
                    if tt == 3:
                        if h == 4 and live(b, h, -H):
                            attention_out(b - 1)
                        if h == 12 and live(b, h, H):
                            exp_logits(b + 1)

            def body(b):
                for h in range(H):
                    slot(b, h)

            over_batches(act, body)
            for h in range(H, H + 5):
                slot(B - 1, h)
            attention_out(B - 1)

        @block.tensor
        def _(pe):
            work, side = [None], [None]

            def take(bank, next_reader, value):
                if bank[0] is not None:
                    pe.wait_ge(*bank[0])
                bank[0] = (next_reader, value)

            def product(dst, stationary, moving, finished):
                (s_hi, s_lo), (m_hi, m_lo) = stationary, moving
                nc.tensor.matmul(dst, s_hi, m_hi, start=True, stop=False)
                nc.tensor.matmul(dst, s_hi, m_lo, start=False, stop=False)
                nc.tensor.matmul(dst, s_lo, m_hi, start=False, stop=True).then_inc(finished, 1)

            def weight(a, n):
                return w_hi[:, a:a + n], w_lo[:, a:a + n]

            def tokens(a, n):
                return xt_hi[:, a:a + n], xt_lo[:, a:a + n]

            def transpose_xn(b):
                take(work, xt_lo_set, b + 1)
                pe.wait_ge(xn_set, b + 1)
                for t in range(T):
                    last = nc.tensor.transpose(work_ps[:, t * P:(t + 1) * P], xn[:, t, :], ident[:, :])
                last.then_inc(xt_up, 1)

            def project_k(b):
                take(side, k_lo_next_set, b + 1)
                pe.wait_ge(xt_hi_set, b + 1)
                pe.wait_ge(xt_lo_set, b + 1)
                product(side_ps[:, :], weight(KK0, 2 * DK), tokens(0, S), k_up)

            def project_v(b):
                take(side, v_t_set, b + 1)
                product(side_ps[0:VR, :], weight(VV0, VR), tokens(0, S), v_up)

            def transpose_v(b):
                take(side, v_next_set, b + 1)
                pe.wait_ge(v_scaled_set, b + 1)
                for t in range(T):
                    last = nc.tensor.transpose(side_ps[:, t * P:t * P + VR], v_scaled[:, t * P:(t + 1) * P],
                                               ident[0:VR, 0:VR])
                last.then_inc(vt_up, 1)

            def project_q(j, p, b_next):
                take(work, q_lo_set, j + 1)
                if p == PAIRS:
                    pe.wait_ge(xt_hi_set, b_next + 1)
                    pe.wait_ge(xt_lo_set, b_next + 1)
                elif isinstance(j, int) and j == 0:
                    pe.wait_ge(xt_hi_set, 1)
                    pe.wait_ge(xt_lo_set, 1)
                product(work_ps[:, :], weight(WQ0 + (p % PAIRS) * P, P), tokens(0, S), q_up)

            def experts(b, item):
                t, half = item // 2, item % 2
                if isinstance(b, int) and b == 0 and item == 0:
                    pe.wait_ge(w_hi_set, 2)
                    pe.wait_ge(w_lo_set, 2)
                take(side, experts_step, (b * (2 * T) + (item + 1)) * HALF)
                product(side_ps[:, :], tokens(t * P, P), weight(WE0 + half * S, S), experts_up)

            def q_full_value(u, h):
                return (u - h % 4) * 20 + 80

            def maxima(u, h, st):
                j2 = (h // 2) % 2
                if st == 0:
                    pe.wait_ge(q_full_in[j2], q_full_value(u, h))
                if not (isinstance(u, int) and u * T + st < 2):
                    pe.wait_ge(max_set, u * T + (st - 1))
                q = q_full_even if h % 2 == 0 else q_full_odd
                k = k_hi_next if h % H < 4 else k_hi
                nc.tensor.matmul(max_ps[:, st % 2, :], q[:, (h // 2) % 4, st * P:(st + 1) * P], k[:, :],
                                 start=True, stop=True).then_inc(max_up, 1)

            def shift_row(u, h):
                take(side, shift_row_set, u + 1)
                pe.wait_ge(max_set, u * T + T)
                nc.tensor.transpose(side_ps[0:T, 0:P], neg_max[:, h % 4, :], ident[:, :]).then_inc(shift_up, 1)

            def scores(u, h, tt):
                if tt == 0:
                    pe.wait_ge(shift_in[h % 2], (u - h % 2) * 8 + 16)
                if not (isinstance(u, int) and u * T + tt < 2):
                    pe.wait_ge(exp_set, u * T + (tt - 1))
                n, keys = (h // 2) % 4, slice(tt * P, (tt + 1) * P)
                full, high, low = ((q_full_even, q_even, k_lo_even) if h % 2 == 0 else (q_full_odd, q_odd, k_lo_odd))
                nc.tensor.matmul(score_ps[:, tt % 2, :], k_hi[:, keys], full[:, n, :], start=True, stop=False)
                nc.tensor.matmul(score_ps[:, tt % 2, :], low[:, keys], high[:, n, :],
                                 start=False, stop=True).then_inc(scores_up, 1)

            def weighted_values(u, h, st):
                if st == 0:
                    pe.wait_ge(e_lo_set, u * T + T)
                    if not (isinstance(u, int) and u == 0):
                        pe.wait_ge(o_pair_set, u)
                queries, a = slice(st * P, (st + 1) * P), st * OW
                for tt in range(T):
                    v_lo = v_cur[:, tt * VS:tt * VS + DK]
                    v_hi = v_cur[:, tt * VS + DK:tt * VS + VW]
                    high, low = e_hi[:, h % 4, tt, queries], e_lo[:, h % 4, tt, queries]
                    nc.tensor.matmul(pv_ps[:, a:a + OW], high, v_hi, start=(tt == 0), stop=False)
                    nc.tensor.matmul(pv_ps[:, a:a + DK], high, v_lo, start=False, stop=False)
                    last = nc.tensor.matmul(pv_ps[:, a:a + OW], low, v_hi, start=False, stop=(tt == T - 1))
                if st == T - 1:
                    last.then_inc(pv_up, 1)

            def transpose_out(j, p):
                take(work, ot_lo_set, j + 1)
                pe.wait_ge(o_pair_set, j * 2 + 2)
                for t in range(T):
                    last = nc.tensor.transpose(work_ps[:, t * P:(t + 1) * P], o_pair[:, p % 2, t, :], ident[:, :])
                last.then_inc(ot_up, 1)

            def project_out(b, j, p):
                if p == 0:
                    if live(b, 0, -H):
                        pe.wait_ge(attn_set, b)
                    else:
                        pe.wait_ge(wo_lo_set, 2)
                pe.wait_ge(ot_lo_set, j + 1)
                w, n = slice(p * D, (p + 1) * D), p % 2
                nc.tensor.matmul(attn_ps[:, :], wo_hi[:, w], ot_hi[:, n, :], start=(p == 0), stop=False)
                nc.tensor.matmul(attn_ps[:, :], wo_hi[:, w], ot_lo[:, n, :], start=False, stop=False)
                last = nc.tensor.matmul(attn_ps[:, :], wo_lo[:, w], ot_hi[:, n, :],
                                        start=False, stop=(p == PAIRS - 1))
                if p == PAIRS - 1:
                    last.then_inc(wo_up, 1)

            def transpose_final(b):
                take(work, final_set, b + 1)
                pe.wait_ge(attn_set, b + 1)
                for t in range(T):
                    last = nc.tensor.transpose(work_ps[:, t * P:(t + 1) * P], attn_t[:, t * P:(t + 1) * P],
                                               ident[:, :])
                last.then_inc(final_up, 1)

            pe.wait_ge(ident_set, 1)
            transpose_xn(0)
            pe.wait_ge(w_hi_set, 1)
            pe.wait_ge(w_lo_set, 1)
            project_q(0, 0, 0)
            project_k(0)
            project_q(1, 1, 0)
            project_v(0)
            transpose_v(0)
            project_q(2, 2, 0)
            pe.wait_ge(k_hi_next_set, 1)
            for st in range(T):
                maxima(0, 0, st)
            shift_row(0, 0)
            for st in range(T):
                maxima(1, 1, st)

            def slot(b, h):
                u = b * H + h
                if h == 14 and live(b, h, 2):
                    pe.wait_ge(k_hi_next_set, b + 2)
                for tt in range(T):
                    if h == 0 and tt % 2 == 0:
                        pe.wait_ge(k_hi_set, b * 2 + (tt // 2 + 1))
                        pe.wait_ge(k_lo_set, b * 2 + (tt // 2 + 1))
                    if live(b, h, 0):
                        scores(u, h, tt)
                    if tt == 1 and live(b, h, 1):
                        shift_row(u + 1, h + 1)
                    if live(b, h, 2):
                        maxima(u + 2, h + 2, tt)
                    if h == 2 and tt == 1 and live(b, h, 0):
                        pe.wait_ge(v_cur_set, b + 1)
                    if live(b, h, -2):
                        for st in ((), (0, 1), (), (2, 3))[tt]:
                            weighted_values(u - 2, h - 2, st)
                    if tt == 2:
                        if 2 <= h < 2 + EXPERTS and live(b, h, 0):
                            experts(b, h - 2)
                        if h == 11 and live(b, h, H):
                            project_v(b + 1)
                        if h == 12 and live(b, h, H):
                            transpose_v(b + 1)
                        if h == 13 and live(b, h, H):
                            project_k(b + 1)
                        if h % 2 == 0 and live(b, h, -4):
                            transpose_out(b * PAIRS + (h - 4) // 2, (h - 4) // 2)
                    if tt == 0:
                        if h == 10 and live(b, h, H):
                            transpose_xn(b + 1)
                        if h % 2 == 0 and live(b, h, -6):
                            p = (h - 6) // 2
                            project_out(b if p >= 0 else b - 1, b * PAIRS + p, p % PAIRS)
                        if h == 6 and live(b, h, -H):
                            transpose_final(b - 1)
                        if h % 2 == 1 and live(b, h, 5):
                            p = (h + 1) // 2 + 2
                            project_q(b * PAIRS + p, p, b + 1)

            def body(b):
                if isinstance(b, int) and b == 0:
                    work[0], side[0] = (q_lo_set, 3), (shift_row_set, 1)
                else:
                    work[0], side[0] = (q_lo_set, b * PAIRS + 3), (shift_row_set, b * H + 1)
                for h in range(H):
                    slot(b, h)

            over_batches(pe, body)
            for h in range(H, H + 5):
                slot(B - 1, h)
            transpose_final(B - 1)

        @block.vector
        def _(dve):
            gate = [0, 0]

            def step(ins):
                gate[1] += 1
                ins.then_inc(gate_step, 1)
                dve.wait_ge(gate_step, gate[0] * GATE_STEPS + gate[1])

            def begin(b, done):
                gate[:] = b, done

            def wide(a):
                return a.rearrange("p (t o) -> p t o", o=1).broadcast_to([P, T, EXPERTS])

            def ln_statistics(tiles):
                for t in tiles:
                    last = nc.vector.bn_stats(stats[:, t, :], x_sb[:, t * D:(t + 1) * D])
                last.then_inc(stats_set, 1)

            def ln_moments(n, tiles):
                dve.wait_ge(stats_set, n + 1)
                for t in tiles:
                    last = nc.vector.bn_aggr(moments[:, t, :], stats[:, t, :])
                last.then_inc(moments_set, 1)

            def ln_guess(n, tiles, groups):
                first = n * LN_STEPS
                dve.wait_ge(moments_set, groups)
                a = slice(tiles[0], tiles[-1] + 1)
                nc.vector.tensor_copy(mean[:, a], moments[:, a, 0])
                nc.vector.tensor_scalar(var_eps[:, a], moments[:, a, 1], LN_EPS, None, ALU.add).then_inc(ln_step, 1)
                dve.wait_ge(ln_step, first + 1)
                nc.vector.tensor_scalar(half_bits[:, a], var_eps[:, a].bitcast(I32), 1, None,
                                        ALU.arith_shift_right).then_inc(ln_step, 1)
                dve.wait_ge(ln_step, first + 2)
                nc.vector.tensor_scalar(guess[:, 0, a], half_bits[:, a], -1.0, float(RSQRT_MAGIC), ALU.mult,
                                        ALU.add).then_inc(ln_step, 1)

            def ln_newton(n, tiles, i):
                first = n * LN_STEPS + 3 * i + 3
                dve.wait_ge(ln_step, first)
                a = slice(tiles[0], tiles[-1] + 1)
                y, y_next = guess[:, i, a].bitcast(F32), guess[:, i + 1, a].bitcast(F32)
                nc.vector.tensor_tensor(newton[:, 0, a], y, y, ALU.mult).then_inc(ln_step, 1)
                dve.wait_ge(ln_step, first + 1)
                nc.vector.scalar_tensor_tensor(out=newton[:, 1, a], in0=newton[:, 0, a], scalar=-0.5,
                                               in1=var_eps[:, a], op0=ALU.mult, op1=ALU.mult).then_inc(ln_step, 1)
                dve.wait_ge(ln_step, first + 2)
                nc.vector.scalar_tensor_tensor(out=y_next, in0=newton[:, 1, a], scalar=1.5, in1=y,
                                               op0=ALU.add, op1=ALU.mult).then_inc(ln_step, 1)

            def ln_to_come(h, tt):
                second, rest = range(T, 2 * T), range(2 * T, B * T)
                if (h, tt) == (1, 3):
                    ln_guess(1, second, 2)
                if (h, tt) in ((3, 3), (4, 1), (5, 3)):
                    ln_newton(1, second, h - 3)
                n, pairs = h - 2, len(rest) // 2
                if tt == 0 and n == 0:
                    dve.wait_ge(x_rest_in, 16 * (B - 2))
                if tt == 0 and 0 <= n < pairs:
                    ln_statistics(rest[2 * n:2 * n + 2])
                if tt == 0 and 0 <= n - 1 < pairs:
                    ln_moments(2 + n - 1, rest[2 * n - 2:2 * n])
                if (h, tt) == (14, 2):
                    ln_guess(2, rest, 2 + pairs)
                if (h, tt) in ((14, 3), (15, 0), (15, 3)):
                    ln_newton(2, rest, {(14, 3): 0, (15, 0): 1, (15, 3): 2}[h, tt])

            def normalise(b, tiles):
                if tiles[0] == 0:
                    groups = b + 1 if isinstance(b, int) and b < 2 else 3
                    dve.wait_ge(ln_step, groups * LN_STEPS)
                    if isinstance(b, int):
                        tokens = slice(b * T, (b + 1) * T)
                    else:
                        tokens = bass.ds(b * T, T)
                    nc.vector.tensor_copy(mean_cur[:, :], mean[:, tokens])
                    nc.vector.tensor_copy(inv_cur[:, :],
                                          guess[:, NEWTON, tokens].bitcast(F32)).then_inc(ln_cur_set, 1)
                    dve.wait_ge(ln_cur_set, b + 1)
                for t in tiles:
                    last = nc.vector.tensor_scalar(xn[:, t, :], x_sb[:, bass.ds((b * T + t) * D, D)],
                                                   mean_cur[:, t:t + 1], inv_cur[:, t:t + 1], ALU.subtract, ALU.mult)
                if t == T - 1:
                    last.then_inc(xn_set, 1)

            def low_weights(n, a, z):
                dve.wait_ge(w_hi_set, n)
                nc.vector.tensor_tensor(w_lo[:, a:z], w_raw[:, a:z], w_hi[:, a:z].bitcast(F32),
                                        ALU.subtract).then_inc(w_lo_set, 1)

            def xt_low(b):
                dve.wait_ge(xt_hi_set, b + 1)
                nc.vector.tensor_tensor(xt_lo[:, :], work_ps[:, :], xt_hi[:, :].bitcast(F32),
                                        ALU.subtract).then_inc(xt_lo_set, 1)

            def k_low(b):
                dve.wait_ge(k_hi_next_set, b + 1)
                nc.vector.scalar_tensor_tensor(out=k_lo_next[:, :], in0=side_ps[:, :], scalar=cols[:, BK0:BK0 + 1],
                                               in1=k_hi_next[:, :].bitcast(F32), op0=ALU.add,
                                               op1=ALU.subtract).then_inc(k_lo_next_set, 1)

            def k_current(b, half):
                if live(b, 0, -H):
                    dve.wait_ge(scores_up, b * (H * T) + (2 * half - 2))
                dve.wait_ge(k_lo_next_set, b + 1)
                keys = slice(half * (S // 2), (half + 1) * (S // 2))
                nc.vector.tensor_copy(k_lo_even[0:DK, keys], k_lo_next[0:DK, keys].bitcast(F32))
                nc.vector.tensor_copy(k_lo_odd[DK:P, keys], k_lo_next[DK:P, keys].bitcast(F32)).then_inc(k_lo_set, 1)

            def v_largest(b):
                if isinstance(b, int) and b == 0:
                    dve.wait_ge(consts_set, 7)
                dve.wait_ge(v_t_set, b + 1)
                nc.vector.tensor_reduce(v_absmax[:, :], v_t[0:DK, :], AX.X, ALU.max,
                                        apply_absolute_value=True).then_inc(v_step, 1)

            def scale_v(b):
                dve.wait_ge(v_step, b * 3 + 1)
                nc.vector.tensor_scalar(v_unit_next[0:DK, :], v_absmax[:, :], 1e-30, 1.0 / VALUE_TOP, ALU.max,
                                        ALU.mult).then_inc(v_step, 1)
                dve.wait_ge(v_step, b * 3 + 2)
                nc.vector.reciprocal(v_scale[0:DK, :], v_unit_next[0:DK, :]).then_inc(v_step, 1)
                dve.wait_ge(v_step, b * 3 + 3)
                nc.vector.tensor_scalar(v_scaled[:, :], v_t[:, :], v_scale[:, 0:1], None,
                                        ALU.mult).then_inc(v_scaled_set, 1)

            def v_low(b):
                nxt = v_next[:, :].rearrange("p (t c) -> p t c", t=T)
                nc.vector.tensor_tensor(nxt[:, :, 0:DK],
                                        side_ps[:, :].rearrange("p (t c) -> p t c", t=T)[:, :, 0:DK],
                                        nxt[:, :, DK:2 * DK], ALU.subtract).then_inc(v_next_set, 1)

            def v_current(b):
                if live(b, 0, -H):
                    dve.wait_ge(pv_up, b * H)
                nc.vector.tensor_copy(v_cur[:, :], v_next[:, :]).then_inc(v_cur_set, 1)

            def shift_logits(b):
                dve.wait_ge(v_hi_set, b + 1)
                source = side_ps[:, :].rearrange("p (t c) -> p t c", t=T)[:, :, DK:VR]
                begin(b, 0)
                step(nc.vector.tensor_reduce(small[:, 0, :], source, AX.X, ALU.max))
                nc.vector.tensor_tensor(logits[:, :, :], source, wide(small[:, 0, :]),
                                        ALU.subtract).then_inc(shifted_set, 1)

            def row(i):
                return small[:, i, :]

            def rows(i, n=2):
                return small[:, i:i + n, :].rearrange("p r t -> p (r t)")

            def gates_softmax(b):
                dve.wait_ge(exp_logits_set, b + 1)
                begin(b, 1)
                step(nc.vector.tensor_reduce(row(2), probs[:, 0, :, :], AX.X, ALU.add))
                step(nc.vector.reciprocal(row(3), row(2)))
                step(nc.vector.tensor_tensor(probs[:, 1, :, :], probs[:, 0, :, :], wide(row(3)), ALU.mult))
                step(nc.vector.tensor_reduce(row(4), probs[:, 1, :, :], AX.X, ALU.max))

            def choose(n, source, largest):
                step(nc.vector.tensor_tensor(gate_parts[:, 0, :, :], source, wide(largest), ALU.is_equal))
                step(nc.vector.tensor_tensor(gate_parts[:, 1, :, :], gate_parts[:, 0, :, :], rank[:, :, :], ALU.mult))
                step(nc.vector.tensor_reduce(row(1), gate_parts[:, 1, :, :], AX.X, ALU.max))
                step(nc.vector.tensor_tensor(onehot[:, n, :, :], rank[:, :, :], wide(row(1)), ALU.is_equal))

            def gates_first(b):
                begin(b, 5)
                choose(0, probs[:, 1, :, :], row(4))

            def gates_second(b):
                begin(b, 9)
                step(nc.vector.scalar_tensor_tensor(out=probs[:, 2, :, :], in0=onehot[:, 0, :, :], scalar=-2.0,
                                                    in1=probs[:, 1, :, :], op0=ALU.mult, op1=ALU.add))
                step(nc.vector.tensor_reduce(row(5), probs[:, 2, :, :], AX.X, ALU.max))
                step(nc.vector.scalar_tensor_tensor(out=row(6), in0=row(4), scalar=MOE_EPS, in1=row(5),
                                                    op0=ALU.add, op1=ALU.add))
                step(nc.vector.reciprocal(row(7), row(6)))

            def gates_chosen(b):
                begin(b, 13)
                choose(1, probs[:, 2, :, :], row(5))

            def gates_weights(b):
                begin(b, 17)
                r = small[:, 7:8, :].broadcast_to([P, 2, T])
                step(nc.vector.tensor_tensor(small[:, 8:10, :], small[:, 4:6, :], r, ALU.mult))
                step(nc.vector.tensor_tensor(row(10), row(8), row(9), ALU.add))
                nc.vector.tensor_scalar(row(11), row(10), MOE_EPS, None, ALU.max)
                step(nc.vector.tensor_scalar(row(12), row(10), MOE_EPS, 1.0, ALU.mult, ALU.add))

            def gates_factor(b):
                begin(b, 20)
                step(nc.vector.reciprocal(row(13), row(11)))
                step(nc.vector.tensor_tensor(row(14), row(13), row(12), ALU.mult))
                f = small[:, 14:15, :].broadcast_to([P, 2, T])
                step(nc.vector.tensor_tensor(small[:, 16:18, :], small[:, 8:10, :], f, ALU.mult))

            def gates_spread(b):
                begin(b, 23)
                both = rows(16).rearrange("p (t o) -> p t o", o=1).broadcast_to([P, 2 * T, EXPERTS])
                step(nc.vector.tensor_tensor(gate_parts[:, :, :, :].rearrange("p a t e -> p (a t) e"),
                                             onehot[:, :, :, :].rearrange("p a t e -> p (a t) e"), both, ALU.mult))
                nc.vector.tensor_tensor(gates[:, :, :], gate_parts[:, 0, :, :], gate_parts[:, 1, :, :],
                                        ALU.add).then_inc(gates_set, 1)
                dve.wait_ge(gates_set, b + 1)
                assert gate[1] == GATE_STEPS, gate

            def experts(b, item, few):
                t, half = item // 2, item % 2
                if few[0] == 0:
                    dve.wait_ge(experts_up, b * (2 * T) + (item + 1))
                acc = x_sb[:, bass.ds((b * T + t) * D, D)]
                for e in few:
                    done = (b * (2 * T) + item) * HALF + e
                    if not (isinstance(done, int) and done == 0):
                        dve.wait_ge(experts_step, done)
                    nc.vector.scalar_tensor_tensor(
                        out=acc, in0=side_ps[:, e * D:(e + 1) * D],
                        scalar=gates[:, t, half * HALF + e:half * HALF + e + 1],
                        in1=acc, op0=ALU.mult, op1=ALU.add).then_inc(experts_step, 1)

            def q_low(j, p):
                dve.wait_ge(q_hi_set, j + 1)
                nc.vector.scalar_tensor_tensor(out=q_lo[:, p % 2, :], in0=work_ps[:, :],
                                               scalar=cols[:, BQ0 + p % PAIRS:BQ0 + p % PAIRS + 1],
                                               in1=q_even[:, p % 4, :].bitcast(F32), op0=ALU.add,
                                               op1=ALU.subtract).then_inc(q_lo_set, 1)

            def maxima(u, h, st):
                dve.wait_ge(max_up, u * T + (st + 1))
                nc.vector.tensor_reduce(neg_max[:, h % 4, st:st + 1], max_ps[:, st % 2, :], AX.X, ALU.max,
                                        negate=True).then_inc(max_set, 1)

            def shift_row(u, h):
                dve.wait_ge(shift_up, u + 1)
                nc.vector.tensor_scalar(shift_rows[:, h % 2, :], side_ps[0:T, 0:P], LN_EXP_TOP / SCALE, None,
                                        ALU.add).then_inc(shift_row_set, 1)

            weighted = pv_ps[:, 0:T * OW].rearrange("p (t c) -> p t c", t=T)

            def invert_denominators(u, h):
                dve.wait_ge(pv_up, u + 1)
                nc.vector.reciprocal(recip[:, h % 2, :].rearrange("p (t o) -> p t o", o=1),
                                     weighted[:, :, DK:OW]).then_inc(recip_set, 1)

            def normalise_out(u, h):
                dve.wait_ge(recip_set, u + 1)
                head = slice((h % 2) * DK, (h % 2) * DK + DK)
                r = recip[:, h % 2, :].rearrange("p (t o) -> p t o", o=1).broadcast_to([P, T, DK])
                nc.vector.tensor_tensor(o_pair[:, (h // 2) % 2, :, head], weighted[:, :, 0:DK], r,
                                        ALU.mult).then_inc(o_pair_set, 1)

            def ot_low(j, p):
                dve.wait_ge(ot_hi_set, j + 1)
                nc.vector.scalar_tensor_tensor(out=ot_lo[:, p % 2, :], in0=work_ps[:, :], scalar=v_unit[:, 0:1],
                                               in1=ot_hi[:, p % 2, :].bitcast(F32), op0=ALU.mult,
                                               op1=ALU.subtract).then_inc(ot_lo_set, 1)

            def final(b):
                dve.wait_ge(final_up, b + 1)
                acc = x_sb[:, bass.ds(b * (T * D), T * D)]
                nc.vector.tensor_tensor(acc, work_ps[:, :], acc, ALU.add).then_inc(final_set, 1)

            dve.wait_ge(x_in, 16)
            ln_statistics(range(T))
            ln_moments(0, range(T))
            ln_guess(0, range(T), 1)
            for i in range(NEWTON):
                ln_newton(0, range(T), i)
            normalise(0, range(T))
            low_weights(1, 0, WE0)
            dve.wait_ge(cols_in, 16)
            dve.wait_ge(consts_set, 8)
            for t in range(T):
                last = nc.vector.tensor_copy(rank[:, t, :], cols[:, RANK0:RANK0 + EXPERTS])
            last.then_inc(rank_set, 1)
            dve.wait_ge(rank_set, 1)
            xt_low(0)
            q_low(0, 0)
            k_low(0)
            k_current(0, 0)
            k_current(0, 1)
            q_low(1, 1)
            v_largest(0)
            scale_v(0)
            dve.wait_ge(x_second_in, 16)
            ln_statistics(range(T, 2 * T))
            ln_moments(1, range(T, 2 * T))
            shift_logits(0)
            v_low(0)
            gates_softmax(0)
            gates_first(0)
            for st in range(T):
                maxima(0, 0, st)
            shift_row(0, 0)
            q_low(2, 2)
            for st in range(T):
                maxima(1, 1, st)
            low_weights(2, WE0, WCOLS)
            gates_second(0)

            gate_pieces = (gates_softmax, gates_first, gates_second, gates_chosen, gates_weights, gates_factor,
                           gates_spread)
            pieces_at = {(13, 1): 0, (14, 1): 1, (15, 1): 2, (0, 1): 3, (0, 2): 4, (1, 1): 5, (2, 1): 6}

            def slot(b, h):
                u = b * H + h
                if h == 2 and live(b, h, 0):
                    v_current(b)
                item = h - 2
                if live(b, h, -3):
                    invert_denominators(u - 3, h - 3)
                if 0 < item <= 2 * T and live(b, h, 0):
                    experts(b, item - 1, (3,))
                if live(b, h, -3):
                    normalise_out(u - 3, h - 3)
                for tt in range(T):
                    if tt == 1 and live(b, h, 1):
                        shift_row(u + 1, h + 1)
                    if tt == 1 and 6 <= h < 6 + T and live(b, h, H):
                        normalise(b + 1, (h - 6,))
                    if tt == 1 and h == 10 and live(b, h, H):
                        xt_low(b + 1)
                    if tt == 1 and h == 12 and live(b, h, H):
                        scale_v(b + 1)
                    if tt == 2 and h == 15 and live(b, h, 1):
                        k_current(b + 1, 0)
                    if tt == 2 and h % 2 == 1 and live(b, h, 5):
                        p = (h + 1) // 2 + 2
                        q_low(b * PAIRS + p, p)
                    if tt == 3:
                        if 0 <= item < 2 * T and live(b, h, 0):
                            experts(b, item, (2,))
                        if h % 2 == 0 and live(b, h, -4):
                            ot_low(b * PAIRS + (h - 4) // 2, (h - 4) // 2)
                        if h == 12 and live(b, h, H):
                            shift_logits(b + 1)
                            v_low(b + 1)
                        if h == 13 and live(b, h, H):
                            k_low(b + 1)
                    if isinstance(b, int) and b == 0:
                        ln_to_come(h, tt)
                        if (h, tt) in ((3, 1), (5, 1)):
                            half = slice((h - 3) // 2 * PAIRS * D // 2, (h - 1) // 2 * PAIRS * D // 2)
                            dve.wait_ge(wo_hi_set, 1)
                            nc.vector.tensor_tensor(wo_lo[:, half], wo_raw[:, half], wo_hi[:, half].bitcast(F32),
                                                    ALU.subtract).then_inc(wo_lo_set, 1)
                    if (h, tt) in pieces_at and live(b, h, H if h > 2 else 0):
                        gate_pieces[pieces_at[h, tt]](b + 1 if h > 2 else b)
                    if live(b, h, 2):
                        maxima(u + 2, h + 2, tt)
                    if tt == 0 and h == 6 and live(b, h, -H):
                        final(b - 1)
                    if tt == 0 and h == 12 and live(b, h, H):
                        v_largest(b + 1)
                    if tt == 2 and 0 <= item < 2 * T and live(b, h, 0):
                        experts(b, item, (0, 1))
                    if tt == 3 and h == 15 and live(b, h, 1):
                        k_current(b + 1, 1)

            def body(b):
                for h in range(H):
                    slot(b, h)

            over_batches(dve, body)
            for h in range(H, H + 4):
                slot(B - 1, h)
            final(B - 1)


_OUT = (B, S, D)


def kernel(**inputs):
    import numpy as np
    import concourse.bacc as bacc
    from concourse.bass_utils import run_bass_kernel_spmd

    g = {k.removeprefix("L0_attn_").removeprefix("L0_ffn_"): np.asarray(v) for k, v in inputs.items()}
    weights = np.concatenate([g["Wk"], g["Wk"], g["Wv"], g["router_w"].T, g["Wq"],
                              g["expert_weights"].transpose(1, 0, 2).reshape(D, EXPERTS * D)], axis=1)
    wo = g["Wo"].reshape(PAIRS, P, D).transpose(1, 0, 2).reshape(P, PAIRS * D)
    columns = np.concatenate([
        g["bq"].reshape(PAIRS, P).T, np.tile(g["bk"], 2)[:, None],
        np.concatenate([g["bv"], g["router_b"], np.zeros(P - VR, np.float32)])[:, None], g["bo"][:, None],
        np.broadcast_to(np.arange(EXPERTS, 0, -1, dtype=np.float32), (P, EXPERTS))], axis=1)
    arrays = {"x": g["x"], "weights": weights, "wo": wo, "columns": columns}
    arrays = {n: np.ascontiguousarray(a) for n, a in arrays.items()}

    nc = bacc.Bacc("TRN2", target_bir_lowering=False, num_devices=1)
    args = [nc.dram_tensor(f"in_{n}", a.shape, F32, kind="ExternalInput").ap() for n, a in arrays.items()]
    args.append(nc.dram_tensor("out_0", _OUT, F32, kind="ExternalOutput").ap())
    build(nc, *args)
    r = run_bass_kernel_spmd(nc, [{f"in_{n}": a for n, a in arrays.items()}], core_ids=[0])
    return r.results[0]["out_0"]
```
